# Optimizing a Trainium2 kernel written in Bass

```python
import numpy as np
import jax
import jax.numpy as jnp

def _softmax(x, axis=-1):
    return jax.nn.softmax(x, axis=axis)

def _gelu(x):
    return jax.nn.gelu(x, approximate=True)

def _silu(x):
    return jax.nn.silu(x)

def _sigmoid(x):
    return jax.nn.sigmoid(x)

def _layernorm(x, axis=-1, eps=1e-05):
    m = jnp.mean(x, axis=axis, keepdims=True)
    v = jnp.var(x, axis=axis, keepdims=True)
    return (x - m) / jnp.sqrt(v + eps)

def _scatter_add(tgt, idx, src, axis=0):
    return tgt.at[idx].add(src)

def _segment_sum(src, seg, n):
    return jax.ops.segment_sum(src, seg, n)
kernel_name = 'mk_flamingo_gated_d1_seqx_r4_3967c9'

def setup_inputs(seed: int=0):
    np.random.seed(seed)
    _w = jnp.asarray

    def _rec_inputs():
        import jax
        import jax.numpy as jnp
        _rk = jax.random.key(seed)
        x = -0.0002928 + 1 * jax.random.normal(jax.random.fold_in(_rk, 1), (4, 1024, 256), jnp.float32)
        _lenS = 1024 - jax.random.randint(jax.random.fold_in(_rk, 7), (4,), 0, max(1, 1024 // 4) + 1, jnp.int32)
        _lenS2 = 77 - jax.random.randint(jax.random.fold_in(_rk, 8), (4,), 0, max(1, 77 // 4) + 1, jnp.int32)
        _ctx_1024P = jax.random.normal(jax.random.fold_in(_rk, 11), (4, 16, 256), jnp.float32)
        _ctx_1024c = jax.random.dirichlet(jax.random.fold_in(_rk, 511), 0.3 * jnp.ones((16,), jnp.float32), (4, 77))
        _ctx_1024t = jnp.einsum('bsk,bkd->bsd', _ctx_1024c, _ctx_1024P)
        _ctx_1024t = _ctx_1024t * jax.lax.rsqrt(jnp.mean(jnp.square(_ctx_1024t)) + 1e-12) * 0.953939
        ctx_1024 = -1.39393e-06 + 0.999914 * (_ctx_1024t + 0.3 * jax.random.normal(jax.random.fold_in(_rk, 611), (4, 77, 256), jnp.float32))
        _validS = jnp.arange(1024)[None, :] < _lenS[:, None]
        _validS2 = jnp.arange(77)[None, :] < _lenS2[:, None]
        _causal = jnp.tril(jnp.ones((1024, 1024), dtype=bool))
        mask_B_ik0 = jnp.where(jnp.ones((4,), dtype=bool), 68, 1563).astype(jnp.int32)
        _g = jax.random.normal(jax.random.fold_in(_rk, 9001), (2, 1), jnp.float32)
        _g = jnp.sign(_g) * jnp.maximum(jnp.abs(_g), 1.0) + (_g == 0) * 1.0
        g_xattn = _g[0]
        g_ffn = _g[1]
        return (x, ctx_1024, mask_B_ik0, g_xattn, g_ffn)
    x, ctx_1024, mask_B_ik0, g_xattn, g_ffn = _rec_inputs()

    def _L0_xattn_setup():
        import jax, jax.numpy as jnp
        import numpy as np
        B, S, D, H = (2, 512, 256, 16)
        DH = D // H

        def _split_heads(x):
            b, s, _ = x.shape
            return x.reshape(b, s, H, DH).transpose(0, 2, 1, 3)
        key = jax.random.key(seed)
        k = jax.random.split(key, 8)
        scale = 0.02
        return {'queries': jax.random.normal(k[0], (B, S, D), dtype=jnp.float32), 'keys': jax.random.normal(k[1], (B, S, D), dtype=jnp.float32), 'values': jax.random.normal(k[2], (B, S, D), dtype=jnp.float32), 'valid_length': jax.random.randint(k[3], (B,), 0, S, dtype=jnp.int64), 'Wq': jax.random.normal(k[4], (D, D), dtype=jnp.float32) * scale, 'Wk': jax.random.normal(k[5], (D, D), dtype=jnp.float32) * scale, 'Wv': jax.random.normal(k[6], (D, D), dtype=jnp.float32) * scale, 'Wo': jax.random.normal(k[7], (D, D), dtype=jnp.float32) * scale}
    _L0_xattn_all = _L0_xattn_setup()
    _L0_xattn_in = {k: v for k, v in _L0_xattn_all.items() if k in ('Wq', 'Wk', 'Wv', 'Wo')}
    del _L0_xattn_all

    def _L0_ffn_setup():
        import jax, jax.numpy as jnp
        import numpy as np
        EMB = 256
        FF = 4 * EMB

        def _ternary(w):
            scale = jnp.maximum(jnp.mean(jnp.abs(w)), 1e-08)
            w_t = jnp.clip(jnp.round(w / scale), -1.0, 1.0)
            return w + jax.lax.stop_gradient(w_t - w)
        key = jax.random.key(seed)
        kx, k1, k2, kb1, kb2 = jax.random.split(key, 5)
        x = jax.random.normal(kx, (4, 512, EMB), dtype=jnp.float32)
        lim1 = 1.0 / np.sqrt(EMB)
        lim2 = 1.0 / np.sqrt(FF)
        W1 = jax.random.uniform(k1, (FF, EMB), jnp.float32, -lim1, lim1)
        b1 = jax.random.uniform(kb1, (FF,), jnp.float32, -lim1, lim1)
        W2 = jax.random.uniform(k2, (EMB, FF), jnp.float32, -lim2, lim2)
        b2 = jax.random.uniform(kb2, (EMB,), jnp.float32, -lim2, lim2)
        return {'x': x, 'W1': W1, 'b1': b1, 'W2': W2, 'b2': b2}
    _L0_ffn_all = _L0_ffn_setup()
    _L0_ffn_in = {k: v for k, v in _L0_ffn_all.items() if k in ('W1', 'b1', 'W2', 'b2')}
    del _L0_ffn_all
    return {'x': x, 'ctx_1024': ctx_1024, 'mask_B_ik0': mask_B_ik0, 'g_xattn': g_xattn, 'g_ffn': g_ffn, 'L0_xattn_Wq': _L0_xattn_in['Wq'], 'L0_xattn_Wk': _L0_xattn_in['Wk'], 'L0_xattn_Wv': _L0_xattn_in['Wv'], 'L0_xattn_Wo': _L0_xattn_in['Wo'], 'L0_ffn_W1': _L0_ffn_in['W1'], 'L0_ffn_b1': _L0_ffn_in['b1'], 'L0_ffn_W2': _L0_ffn_in['W2'], 'L0_ffn_b2': _L0_ffn_in['b2']}

def reference(x, ctx_1024, mask_B_ik0, g_xattn, g_ffn, L0_xattn_Wq, L0_xattn_Wk, L0_xattn_Wv, L0_xattn_Wo, L0_ffn_W1, L0_ffn_b1, L0_ffn_W2, L0_ffn_b2):
    import jax
    import jax.numpy as jnp

    def _L0_xattn_ref(queries, keys, values, valid_length, Wq, Wk, Wv, Wo):
        import jax, jax.numpy as jnp
        import numpy as np
        B, S, D, H = (2, 512, 256, 16)
        DH = D // H

        def _split_heads(x):
            b, s, _ = x.shape
            return x.reshape(b, s, H, DH).transpose(0, 2, 1, 3)
        q = _split_heads(queries @ Wq)
        k = _split_heads(keys @ Wk)
        v = _split_heads(values @ Wv)
        scores = jnp.einsum('bhqd,bhkd->bhqk', q, k)
        attn = jax.nn.softmax(scores, axis=-1)
        out = jnp.einsum('bhqk,bhkd->bhqd', attn, v)
        out = out.transpose(0, 2, 1, 3).reshape(queries.shape[0], queries.shape[1], D)
        return out @ Wo

    def _L0_ffn_ref(x, W1, b1, W2, b2):
        import jax, jax.numpy as jnp
        import numpy as np
        EMB = 256
        FF = 4 * EMB

        def _ternary(w):
            scale = jnp.maximum(jnp.mean(jnp.abs(w)), 1e-08)
            w_t = jnp.clip(jnp.round(w / scale), -1.0, 1.0)
            return w + jax.lax.stop_gradient(w_t - w)
        h = jnp.einsum('bsd,fd->bsf', x, _ternary(W1)) + b1
        h = jax.nn.gelu(h, approximate=False)
        out = jnp.einsum('bsf,df->bsd', h, _ternary(W2)) + b2
        return out
    x = x + jnp.tanh(g_xattn[0]) * _L0_xattn_ref(_layernorm(x, axis=-1), ctx_1024, ctx_1024, mask_B_ik0, L0_xattn_Wq, L0_xattn_Wk, L0_xattn_Wv, L0_xattn_Wo)
    x = x + jnp.tanh(g_ffn[0]) * _L0_ffn_ref(_layernorm(x, axis=-1), L0_ffn_W1, L0_ffn_b1, L0_ffn_W2, L0_ffn_b2)
    return x

_drawn_inputs = setup_inputs


def setup_inputs(seed=0):
    import zlib

    import numpy as np

    out = dict(_drawn_inputs(seed))
    spreads = {}
    factors = {'L0_xattn_Wq': 8.0, 'L0_xattn_Wk': 8.0, 'L0_ffn_b1': 23.735, 'L0_ffn_b2': 64.0}
    for name, (base, spread) in spreads.items():
        noise = np.random.default_rng([zlib.crc32(name.encode()), seed]).standard_normal(out[name].shape)
        drawn = base * np.exp(spread * noise) if base else spread * noise
        out[name] = jnp.asarray(drawn.astype(out[name].dtype))
    for name, factor in factors.items():
        out[name] = (out[name] * factor).astype(out[name].dtype)
    return out
```

```python
from contextlib import ExitStack

import concourse.bass as bass
from concourse import mybir

F32 = mybir.dt.float32
F32R = mybir.dt.float32r
BF16 = mybir.dt.bfloat16
ALU = mybir.AluOpType
ACT = mybir.ActivationFunctionType
AX_X = mybir.AxisListType.X

P = 128
HEADS = 16
EPS = 1e-5


def gated_cross_attention_block(nc, x, ctx, g_xattn, g_ffn, Wq, Wk, Wv, Wo, W1, b1, W2, b2, out):
    B, S, D = x.shape
    NK = ctx.shape[1]
    FF = W1.shape[0]
    DH = D // HEADS
    KT = D // P
    HH = P // DH
    FT = FF // P
    BLK = 512
    NB = B * S // BLK
    BPB = S // BLK
    SUB = BLK // P
    HK = HH * NK
    TH = -(-HK // P)
    NT = KT * TH
    ROWS = [min(P, HK - t * P) for t in range(TH)]
    VC = HH * DH + HH
    NMX = SUB * KT
    assert BPB == 2 and NB >= 4 and HK % 2 == 0 and NT % 2 == 0 and FT % 2 == 0

    x_v = x.rearrange("b t d -> (b t) d").rearrange("(n p s) d -> n p (s d)", p=P, s=SUB)
    out_v = out.rearrange("b t d -> (b t) d").rearrange("(n p s) d -> n p (s d)", p=P, s=SUB)

    with ExitStack() as stack:
        def sb(name, shape, dt=F32):
            return stack.enter_context(nc.sbuf_tensor(name, shape, dt))

        def psum(name):
            return stack.enter_context(nc.psum_tensor(name, [P, 512], F32))

        def sem(name):
            return stack.enter_context(nc.semaphore(name))

        ring = [psum("ring0"), psum("ring1")]
        turn = [psum("turn0"), psum("turn1")]
        mxb = [psum("mxb0"), psum("mxb1")]
        o_ps = psum("o_ps")
        y_ps = psum("y_ps")
        ybank = [y_ps, o_ps]

        ident = sb("ident", [P, P])
        ident_b = sb("ident_b", [P, P], BF16)
        ones = sb("ones", [P, P])
        kmask = sb("kmask", [P, HH])
        vmask = sb("vmask", [P, TH, HH])
        headsel = sb("headsel", [2 * HEADS, KT, HK], BF16)
        neg_half = sb("neg_half", [P, SUB])
        Wk_s = sb("Wk_s", [P, KT, D])
        Wv_s = sb("Wv_s", [P, KT, D])
        Wq_s = sb("Wq_s", [P, KT, D])
        Wo_s = sb("Wo_s", [P, KT, D])
        Wq_hi, Wq_lo = sb("Wq_hi", [P, KT, D], F32R), sb("Wq_lo", [P, KT, D], F32R)
        Wo_hi, Wo_lo = sb("Wo_hi", [P, KT, D], F32R), sb("Wo_lo", [P, KT, D], F32R)
        tneg = sb("tneg", [P, FT * D])
        W1T = sb("W1T", [P, KT, FF], F32R)
        W2T = sb("W2T", [P, FT, D], F32R)
        b1_r = sb("b1_r", [FT, P])
        b1_s = sb("b1_s", [P, FT])
        b2_s = sb("b2_s", [P, D])
        b2_g = sb("b2_g", [P, D])
        gates = sb("gates", [P, 2])
        tg = sb("tg", [P, 2])
        wabs = sb("wabs", [P, 2, FT])
        wsum = sb("wsum", [P, 2])
        wscale = sb("wscale", [P, 2])
        thr = sb("thr", [P, 2, 2])

        ctx_s = sb("ctx_s", [NK, D])
        ctxT = sb("ctxT", [P, KT, HK])
        K_f = sb("K_f", [P, KT, HK])
        K_hi, K_lo = sb("K_hi", [P, KT, HK], F32R), sb("K_lo", [P, KT, HK], F32R)
        V_s = sb("V_s", [P, TH, KT, VC])

        xb = [sb(f"xb{i}", [P, SUB, D]) for i in range(2)]
        stats = [sb(f"stats{i}", [P, SUB, 6]) for i in range(2)]
        lnp = [sb(f"lnp{i}", [P, 6, SUB]) for i in range(2)]
        rstd = [sb(f"rstd{i}", [P, SUB]) for i in range(2)]
        xn = [sb(f"xn{i}", [P, SUB, D]) for i in range(2)]
        xT_hi, xT_lo = sb("xT_hi", [P, KT, BLK], F32R), sb("xT_lo", [P, KT, BLK], F32R)
        qT_hi, qT_lo = sb("qT_hi", [P, KT, BLK], F32R), sb("qT_lo", [P, KT, BLK], F32R)
        nm = sb("nm", [P, SUB, HEADS])
        nmb = sb("nmb", [P, SUB, 2 * HEADS], BF16)
        nmT = sb("nmT", [2 * HEADS, BLK], BF16)
        probs = sb("probs", [P, NT, BLK])
        rz = [sb(f"rz{i}", [P, KT, HH]) for i in range(2)]
        o_s = sb("o_s", [P, SUB, D])
        oT_hi, oT_lo = sb("oT_hi", [P, KT, BLK], F32R), sb("oT_lo", [P, KT, BLK], F32R)
        x2 = sb("x2", [P, SUB, D])
        x2T_hi, x2T_lo = sb("x2T_hi", [P, KT, BLK], F32R), sb("x2T_lo", [P, KT, BLK], F32R)
        h_f = sb("h_f", [P, FT, BLK])
        w12 = h_f[:, :, :].rearrange("p f n -> p (f n)")
        W1_s = w12[:, 0:FT * D].rearrange("p (f n) -> p f n", n=D)
        W2_s = w12[:, FT * D:].rearrange("p (k n) -> p k n", n=FF)
        h_hi, h_lo = sb("h_hi", [P, FT, BLK], F32R), sb("h_lo", [P, FT, BLK], F32R)
        y = [sb(f"y{i}", [P, SUB, D]) for i in range(2)]

        in_x = [sem(f"in_x{i}") for i in range(2)]
        in_ctx = sem("in_ctx")
        in_wq, in_wk, in_wv, in_wo = sem("in_wq"), sem("in_wk"), sem("in_wv"), sem("in_wo")
        in_w1, in_w2, in_b1, in_b2, in_g = sem("in_w1"), sem("in_w2"), sem("in_b1"), sem("in_b2"), sem("in_g")
        pool_chain = sem("pool_chain")
        ones_set = sem("ones_set")
        tg_set, b2_set = sem("tg_set"), sem("b2_set")
        wq_hi_set, wq_lo_set, wo_hi_set, wo_lo_set = (sem(f"{w}_set") for w in ("wq_hi", "wq_lo", "wo_hi", "wo_lo"))
        wabs_set, wsum_done, tern_step, tern_set = sem("wabs_set"), sem("wsum_done"), sem("tern_step"), sem("tern_set")
        wt_done, wt_set = sem("wt_done"), sem("wt_set")
        ctxT_done, ctxT_set, kT_done, k_masked, k_hi_set, k_lo_set = (
            sem(s) for s in ("ctxT_done", "ctxT_set", "kT_done", "k_masked", "k_hi_set", "k_lo_set"))
        v_done, v_set, v_ones_set = sem("v_done"), sem("v_set"), sem("v_ones_set")
        st_set, half_set, mean_set, sq_set, var_set, ve_set, rstd_set, xn_set = (
            [sem(f"{s}{i}") for i in range(2)]
            for s in ("st_set", "half_set", "mean_set", "sq_set", "var_set", "ve_set", "rstd_set", "xn_set"))
        xT_done, xT_hi_set, xT_lo_set = sem("xT_done"), sem("xT_hi_set"), sem("xT_lo_set")
        q_done, q_hi_set, q_lo_set = sem("q_done"), sem("q_hi_set"), sem("q_lo_set")
        mx_done, mx_red, nm_hi_set, nm_set = sem("mx_done"), sem("mx_red"), sem("nm_hi_set"), sem("nm_set")
        nmT_done, nmT_set = sem("nmT_done"), sem("nmT_set")
        s_done, exp_done, pv_done, rz_set, o_set = (
            sem(s) for s in ("s_done", "exp_done", "pv_done", "rz_set", "o_set"))
        oT_done, oT_hi_set, oT_lo_set = sem("oT_done"), sem("oT_hi_set"), sem("oT_lo_set")
        wo_done, x2_set, y_base = sem("wo_done"), sem("x2_set"), sem("y_base")
        x2T_done, x2T_hi_set, x2T_lo_set = sem("x2T_done"), sem("x2T_hi_set"), sem("x2T_lo_set")
        f1_done, gelu_done, h_hi_set, h_lo_set, f2_done, y_set = (
            sem(s) for s in ("f1_done", "gelu_done", "h_hi_set", "h_lo_set", "f2_done", "y_set"))
        y_free = [sem(f"y_free{i}") for i in range(2)]

        N_CONST = 13

        def steps(eng, step):
            step(-1, 1, True, False, False, None, 0)
            step(0, 0, True, True, False, 0, None)
            with eng.Fori(0, (NB - 2) // 2) as i:
                step(2 * i + 1, 1, True, True, True, i, i + 1)
                step(2 * i + 2, 0, True, True, True, i + 1, None)
            step(NB - 1, 1, False, True, True, NB // BPB - 1, None)
            step(NB, 0, False, False, True, None, None)

        block = stack.enter_context(nc.Block())

        @block.sync
        def _(sp):
            sp.dma_start(xb[0][:, :, :], x_v[0].rearrange("p (s d) -> p s d", s=SUB)).then_inc(in_x[0], 16)
            sp.dma_start(ctx_s[:, :], ctx[0]).then_inc(in_ctx, 16)
            for w, w_s, w_in in ((Wq, Wq_s, in_wq), (Wk, Wk_s, in_wk), (Wv, Wv_s, in_wv), (Wo, Wo_s, in_wo)):
                sp.dma_start(w_s[:, :, :], w.rearrange("(k p) n -> p k n", p=P)).then_inc(w_in, 16)
            sp.dma_start(gates[:, 0:1], g_xattn.partition_broadcast(P)).then_inc(in_g, 16)
            sp.dma_start(gates[:, 1:2], g_ffn.partition_broadcast(P)).then_inc(in_g, 16)
            sp.dma_start(b2_s[:, :], b2.partition_broadcast(P)).then_inc(in_b2, 16)
            sp.dma_start(b1_r[:, :], b1.rearrange("(f p) -> f p", p=P)).then_inc(in_b1, 16)
            sp.dma_start(xb[1][:, :, :], x_v[1].rearrange("p (s d) -> p s d", s=SUB)).then_inc(in_x[1], 16)
            sp.dma_start(W1_s[:, :, :], W1.rearrange("(f p) n -> p f n", p=P)).then_inc(in_w1, 16)
            sp.dma_start(W2_s[:, :, :], W2.rearrange("(k p) n -> p k n", p=P)).then_inc(in_w2, 16)

            def step(n, par, a, b, c, own, batch):
                first, second = not b and not c, b and not c
                if batch is not None and b:
                    sp.wait_ge(ctxT_done, batch)
                    sp.dma_start(ctx_s[:, :], ctx[batch]).then_inc(in_ctx, 16)
                if c:
                    if a:
                        sp.wait_ge(x2_set, SUB * n)
                        sp.wait_ge(xn_set[0], SUB * n)
                        sp.dma_start(xb[1 - par][:, :, :], x_v[n + 1].rearrange("p (s d) -> p s d", s=SUB)
                                     ).then_inc(in_x[1 - par], 16)
                    sp.wait_ge(y_set, SUB * n)
                    sp.dma_start(out_v[n - 1].rearrange("p (s d) -> p s d", s=SUB), y[1 - par][:, :, :]
                                 ).then_inc(y_free[1 - par], 16)
            steps(sp, step)
            for par in range(2):
                sp.wait_ge(y_free[par], 16 * (NB // 2 + 1))

        @block.gpsimd
        def _(pool):
            done = [0]

            def chain(ins):
                done[0] += 1
                ins.then_inc(pool_chain, 1)
                return done[0]

            def band(t, pattern, width):
                pool.wait_ge(pool_chain, chain(nc.gpsimd.affine_select(
                    out=t, in_=t, pattern=[[-s, c] for s, c in pattern], compare_op=ALU.is_ge, fill=0.0,
                    base=0, channel_multiplier=1)))
                return chain(nc.gpsimd.affine_select(
                    out=t, in_=t, pattern=pattern, compare_op=ALU.is_ge, fill=0.0,
                    base=width - 1, channel_multiplier=-1))

            def diagonal(t, pattern, base):
                return chain(nc.gpsimd.affine_select(
                    out=t, in_=t, pattern=pattern, compare_op=ALU.not_equal, fill=1.0,
                    base=base, channel_multiplier=-1))

            pool.wait_ge(pool_chain, chain(nc.gpsimd.memset(ident[:, :], 0.0)))
            diagonal(ident[:, :], [[1, P]], 0)
            chain(nc.gpsimd.memset(neg_half[:, :], -0.5))
            for i in range(2):
                nc.gpsimd.memset(y[i][:, 0, 0:1], 0.0).then_inc(y_free[i], 16)
            pool.wait_ge(pool_chain, chain(nc.gpsimd.memset(kmask[:, :], 1.0)))
            band(kmask[:, :], [[DH, HH]], DH)

            def inverse_deviation(which, blk):
                pool.wait_ge(ve_set[which], blk + 1)
                nc.gpsimd.tensor_tensor(rstd[which][:, :], lnp[which][:, 5, :], neg_half[:, :], ALU.pow
                                        ).then_inc(rstd_set[which], 1)

            def prepare():
                pool.wait_ge(in_wq, 16)
                pool.wait_ge(wq_hi_set, 1)
                nc.gpsimd.tensor_tensor(Wq_lo[:, :, :], Wq_s[:, :, :], Wq_hi[:, :, :].bitcast(F32), ALU.subtract
                                        ).then_inc(wq_lo_set, 1)
                pool.wait_ge(pool_chain, chain(nc.gpsimd.memset(vmask[:, :, :], 1.0)))
                pool.wait_ge(pool_chain, chain(nc.gpsimd.affine_select(
                    out=vmask[:, :, :], in_=vmask[:, :, :], pattern=[[P, TH], [-NK, HH]], compare_op=ALU.is_ge,
                    fill=0.0, base=0, channel_multiplier=1)))
                chain(nc.gpsimd.affine_select(
                    out=vmask[:, :, :], in_=vmask[:, :, :], pattern=[[-P, TH], [NK, HH]], compare_op=ALU.is_ge,
                    fill=0.0, base=NK - 1, channel_multiplier=-1))
                sel = headsel[:, :, :].rearrange("r k (h m) -> r k h m", h=HH)
                pool.wait_ge(pool_chain, chain(nc.gpsimd.memset(sel, 0.0)))
                pool.wait_ge(pool_chain, diagonal(sel, [[HH, KT], [1, HH], [0, NK]], 0))
                diagonal(sel, [[HH, KT], [1, HH], [0, NK]], HEADS)
                chain(nc.gpsimd.tensor_copy(ident_b[:, :], ident[:, :]))
                assert done[0] == N_CONST, done
                pool.wait_ge(wo_hi_set, 1)
                nc.gpsimd.tensor_tensor(Wo_lo[:, :, :], Wo_s[:, :, :], Wo_hi[:, :, :].bitcast(F32), ALU.subtract
                                        ).then_inc(wo_lo_set, 1)
                pool.wait_ge(in_b2, 16)
                pool.wait_ge(tg_set, 1)
                nc.gpsimd.tensor_scalar(b2_g[:, :], b2_s[:, :], tg[:, 1:2], None, ALU.mult).then_inc(b2_set, 1)

            def step(n, par, a, b, c, own, batch):
                first, second = not b and not c, b and not c
                if a:
                    if first:
                        pool.wait_ge(pool_chain, 3)
                    inverse_deviation(0, n + 1)
                if first:
                    prepare()
                if c:
                    for f in range(FT):
                        pool.wait_ge(h_hi_set, FT * (n - 1) + f + 1)
                        nc.gpsimd.tensor_tensor(h_lo[:, f, :], h_f[:, f, :], h_hi[:, f, :].bitcast(F32), ALU.subtract
                                                ).then_inc(h_lo_set, 1)
                if b:
                    inverse_deviation(1, n)
                    if second:
                        pool.wait_ge(b2_set, 1)
                    if c:
                        pool.wait_ge(y_free[par], 16 * (own + 1))
                    nc.gpsimd.tensor_tensor(y[par][:, :, :], x2[:, :, :],
                                            b2_g[:, :].unsqueeze(1).broadcast_to([P, SUB, D]), ALU.add
                                            ).then_inc(y_base, 1)
            steps(pool, step)

        @block.scalar
        def _(act):
            def copy(dst, src, done):
                nc.scalar.activation(dst, src, ACT.Copy).then_inc(done, 1)

            act.wait_ge(in_wq, 16)
            copy(Wq_hi[:, :, :], Wq_s[:, :, :], wq_hi_set)
            act.wait_ge(in_g, 32)
            nc.scalar.activation(tg[:, :], gates[:, :], ACT.Tanh).then_inc(tg_set, 1)

            def step(n, par, a, b, c, own, batch):
                first, second = not b and not c, b and not c
                def scores(t0, t1):
                    for t in range(t0, t1):
                        rows = ROWS[t % TH]
                        act.wait_ge(s_done, NT * n + t + 1)
                        if c:
                            act.wait_ge(pv_done, SUB * n)
                        nc.scalar.activation(probs[:rows, t, :], ring[t % 2][:rows, :], ACT.Exp
                                             ).then_inc(exp_done, 1)

                if b:
                    scores(0, NT // 2)
                if c:
                    for h in range(KT):
                        act.wait_ge(x2T_done, KT * (n - 1) + h + 1)
                        copy(x2T_hi[:, h, :], turn[h][:, :], x2T_hi_set)
                if b:
                    scores(NT // 2, NT)
                if a:
                    for h in range(KT):
                        act.wait_ge(xT_done, KT * (n + 1) + h + 1)
                        if b:
                            act.wait_ge(q_done, KT * (n + 1))
                        copy(xT_hi[:, h, :], turn[h][:, :], xT_hi_set)

                def gelu(f0, f1):
                    for f in range(f0, f1):
                        act.wait_ge(f1_done, FT * (n - 1) + f + 1)
                        nc.scalar.activation(h_f[:, f, :], ring[f % 2][:, :], ACT.Gelu, bias=b1_s[:, f:f + 1]
                                             ).then_inc(gelu_done, 1)

                if c:
                    gelu(0, 2)
                if a:
                    for h in range(KT):
                        act.wait_ge(q_done, KT * (n + 1) + h + 1)
                        if b:
                            act.wait_ge(s_done, NT * (n + 1))
                            act.wait_ge(mx_done, NMX * (n + 1))
                        copy(qT_hi[:, h, :], turn[h][:, :], q_hi_set)
                if first:
                    act.wait_ge(in_wo, 16)
                    copy(Wo_hi[:, :, :], Wo_s[:, :, :], wo_hi_set)
                if c:
                    gelu(2, FT)
                if second:
                    for g in range(4 * KT):
                        act.wait_ge(wt_done, g + 1)
                        dst = W1T[:, g // 2 % KT, g % 2 * 512:g % 2 * 512 + 512] if g < 2 * KT else (
                            W2T[:, :, :].rearrange("p (q f) (k d) -> p k q f d", q=2, k=KT)[:, (g - 2 * KT) // 2, g % 2])
                        src = ring[g % 2][:, :]
                        if g >= 2 * KT:
                            src = src.rearrange("p (f d) -> p f d", d=P)
                        copy(dst, src, wt_set)
                    act.wait_ge(wt_done, 4 * KT + 1)
                    copy(b1_s[:, :], ring[0][:, 0:FT], wt_set)
                if b:
                    for h in range(KT):
                        act.wait_ge(oT_done, KT * n + h + 1)
                        if c:
                            act.wait_ge(wo_done, SUB * n)
                        copy(oT_hi[:, h, :], turn[h][:, :], oT_hi_set)
            steps(act, step)

        @block.vector
        def _(dve):
            def statistics(which, blk, src):
                diff, total, m2, mean, sq, ve = (lnp[which][:, i, :] for i in range(6))
                for s in range(SUB):
                    nc.vector.bn_stats(stats[which][:, s, :], src[:, s, :]).then_inc(st_set[which], 1)
                dve.wait_ge(st_set[which], SUB * (blk + 1))
                even, odd = stats[which][:, :, 0:3], stats[which][:, :, 3:6]
                nc.vector.tensor_tensor(diff, even[:, :, 1], odd[:, :, 1], ALU.subtract).then_inc(half_set[which], 1)
                nc.vector.tensor_tensor(total, even[:, :, 1], odd[:, :, 1], ALU.add).then_inc(half_set[which], 1)
                nc.vector.tensor_tensor(m2, even[:, :, 2], odd[:, :, 2], ALU.add).then_inc(half_set[which], 1)
                dve.wait_ge(half_set[which], 3 * (blk + 1))
                nc.vector.scalar_tensor_tensor(sq, diff, D / 4, diff, ALU.mult, ALU.mult).then_inc(sq_set[which], 1)
                nc.vector.tensor_scalar(mean, total, 0.5, None, ALU.mult).then_inc(mean_set[which], 1)
                dve.wait_ge(sq_set[which], blk + 1)
                nc.vector.tensor_tensor(diff, sq, m2, ALU.add).then_inc(var_set[which], 1)
                dve.wait_ge(var_set[which], blk + 1)
                nc.vector.tensor_scalar(ve, diff, 1.0 / D, EPS, ALU.mult, ALU.add).then_inc(ve_set[which], 1)

            def normalize(which, blk, src):
                dve.wait_ge(mean_set[which], blk + 1)
                dve.wait_ge(rstd_set[which], blk + 1)
                for s in range(SUB):
                    nc.vector.tensor_scalar(xn[which][:, s, :], src[:, s, :], lnp[which][:, 3, s:s + 1],
                                            rstd[which][:, s:s + 1], ALU.subtract, ALU.mult
                                            ).then_inc(xn_set[which], 1)

            def low_part(dst, hi, blk, hi_set, lo_set):
                for h in range(KT):
                    dve.wait_ge(hi_set, KT * blk + h + 1)
                    nc.vector.tensor_tensor(dst[:, h, :], turn[h][:, :], hi[:, h, :].bitcast(F32), ALU.subtract
                                            ).then_inc(lo_set, 1)

            nc.vector.memset(ones[:, :], 1.0).then_inc(ones_set, 1)
            nc.vector.memset(V_s[:, :, :, :], 0.0).then_inc(v_ones_set, 1)

            def step(n, par, a, b, c, own, batch):
                first, second = not b and not c, b and not c
                def masks_T():
                    dve.wait_ge(ctxT_done, batch + 1)
                    if b:
                        dve.wait_ge(v_done, TH * batch)
                    dst = ctxT[:, :, :].rearrange("p k (h m) -> p k h m", h=HH)
                    for k in range(KT):
                        src = turn[0][:, k * P:k * P + NK].unsqueeze(1).broadcast_to([P, HH, NK])
                        nc.vector.tensor_copy(dst[:, k], src).then_inc(ctxT_set, 1)

                def keys():
                    dve.wait_ge(kT_done, batch + 1)
                    if first:
                        dve.wait_ge(pool_chain, 6)
                    for k in range(KT):
                        src = turn[1][:, k * P:k * P + NK].unsqueeze(1).broadcast_to([P, HH, NK])
                        msk = kmask[:, :].unsqueeze(2).broadcast_to([P, HH, NK])
                        nc.vector.tensor_tensor(K_f[:, k, :].rearrange("p (h m) -> p h m", h=HH), src, msk, ALU.mult
                                                ).then_inc(k_masked, 1)
                    if b:
                        dve.wait_ge(s_done, NT * (n + 1))
                        dve.wait_ge(mx_done, NMX * (n + 1))
                    dve.wait_ge(k_masked, KT * (batch + 1))
                    nc.vector.tensor_copy(K_hi[:, :, :], K_f[:, :, :]).then_inc(k_hi_set, 1)
                    dve.wait_ge(k_hi_set, batch + 1)
                    nc.vector.tensor_tensor(K_lo[:, :, :], K_f[:, :, :], K_hi[:, :, :].bitcast(F32), ALU.subtract
                                            ).then_inc(k_lo_set, 1)

                def values():
                    if b:
                        dve.wait_ge(pv_done, SUB * (n + 1))
                    for t in range(TH):
                        dve.wait_ge(v_done, TH * batch + t + 1)
                        if first and t == 0:
                            dve.wait_ge(pool_chain, N_CONST)
                            dve.wait_ge(v_ones_set, 1)
                        r = ROWS[t]
                        dst = V_s[:r, t, :, 0:HH * DH].rearrange("p k (h d) -> p k h d", h=HH)
                        src = turn[t % 2][:r, 0:D].rearrange("p (k h d) -> p k h d", k=KT, h=HH)
                        msk = vmask[:r, t, :].unsqueeze(1).unsqueeze(3).broadcast_to([r, KT, HH, DH])
                        nc.vector.tensor_tensor(dst, src, msk, ALU.mult).then_inc(v_set, 1)
                    if first:
                        nc.vector.tensor_copy(V_s[:, :, :, HH * DH:VC],
                                              vmask[:, :, :].unsqueeze(2).broadcast_to([P, TH, KT, HH])
                                              ).then_inc(v_ones_set, 1)

                def h_high(f0, f1):
                    for f in range(f0, f1):
                        dve.wait_ge(gelu_done, FT * (n - 1) + f + 1)
                        nc.vector.tensor_copy(h_hi[:, f, :], h_f[:, f, :]).then_inc(h_hi_set, 1)

                def head_outputs(s):
                    dve.wait_ge(pv_done, SUB * n + s + 1)
                    o_v = o_ps[:, 0:KT * VC].rearrange("p (k c) -> p k c", k=KT)
                    nc.vector.reciprocal(rz[s % 2][:, :, :], o_v[:, :, HH * DH:VC]).then_inc(rz_set, 1)
                    dve.wait_ge(rz_set, SUB * n + s + 1)
                    nc.vector.tensor_tensor(
                        o_s[:, s, :].rearrange("p (k h d) -> p k h d", k=KT, h=HH),
                        o_v[:, :, 0:HH * DH].rearrange("p k (h d) -> p k h d", h=HH),
                        rz[s % 2][:, :, :].unsqueeze(3).broadcast_to([P, KT, HH, DH]), ALU.mult).then_inc(o_set, 1)

                def maxima(g):
                    s, h = divmod(g, KT)
                    dve.wait_ge(mx_done, NMX * (n + 1) + g + 1)
                    for i in range(2):
                        ins = nc.vector.tensor_reduce(
                            nm[:, s, h * HH + i * (HH // 2):h * HH + (i + 1) * (HH // 2)],
                            mxb[i][:, 0:HK // 2].rearrange("p (h m) -> p h m", m=NK), AX_X, ALU.max, negate=True)
                    ins.then_inc(mx_red, 1)

                def max_parts():
                    dve.wait_ge(mx_red, NMX * (n + 2))
                    nc.vector.tensor_copy(nmb[:, :, 0:HEADS], nm[:, :, :]).then_inc(nm_hi_set, 1)
                    dve.wait_ge(nm_hi_set, n + 2)
                    nc.vector.tensor_tensor(nmb[:, :, HEADS:], nm[:, :, :], nmb[:, :, 0:HEADS], ALU.subtract
                                            ).then_inc(nm_set, 1)

                def residual(s):
                    dve.wait_ge(wo_done, SUB * n + s + 1)
                    if c and s == 0:
                        dve.wait_ge(xn_set[1], SUB * n)
                        dve.wait_ge(y_base, n)
                    nc.vector.scalar_tensor_tensor(x2[:, s, :], ybank[s % 2][:, 0:D], tg[:, 0:1], xb[par][:, s, :],
                                                   ALU.mult, ALU.add).then_inc(x2_set, 1)

                def mlp_out(s):
                    dve.wait_ge(f2_done, SUB * (n - 1) + s + 1)
                    dve.wait_ge(y_base, n)
                    yv = y[1 - par][:, s, :]
                    nc.vector.scalar_tensor_tensor(yv, ybank[s % 2][:, 0:D], tg[:, 1:2], yv, ALU.mult, ALU.add
                                                   ).then_inc(y_set, 1)

                if a:
                    dve.wait_ge(in_x[1 - par], 16 * ((own if batch is None else batch) + 1))
                    statistics(0, n + 1, xb[1 - par])
                if c:
                    low_part(x2T_lo, x2T_hi, n - 1, x2T_hi_set, x2T_lo_set)
                if a:
                    normalize(0, n + 1, xb[1 - par])
                if first:
                    masks_T()
                    keys()
                if a:
                    low_part(xT_lo, xT_hi, n + 1, xT_hi_set, xT_lo_set)
                if c:
                    h_high(0, 1)
                if b:
                    head_outputs(0)
                if a:
                    low_part(qT_lo, qT_hi, n + 1, q_hi_set, q_lo_set)
                if c:
                    h_high(1, 3)
                if b:
                    head_outputs(1)
                if b and batch is not None:
                    masks_T()
                if c:
                    h_high(3, 5)
                if b:
                    head_outputs(2)
                if b and batch is not None:
                    keys()
                if c:
                    h_high(5, 7)
                if b:
                    head_outputs(3)
                if c:
                    h_high(7, 8)
                if second:
                    dve.wait_ge(in_w1, 16)
                    nc.vector.tensor_reduce(wabs[:, 0, :], W1_s[:, :, :], AX_X, ALU.add,
                                            apply_absolute_value=True).then_inc(wabs_set, 1)
                    dve.wait_ge(in_w2, 16)
                    nc.vector.tensor_reduce(wabs[:, 1, :], W2_s[:, :, :].rearrange("p k (c d) -> p (k c) d", d=D),
                                            AX_X, ALU.add, apply_absolute_value=True).then_inc(wabs_set, 1)
                    dve.wait_ge(wsum_done, 1)
                    chain = 0

                    def link(ins):
                        nonlocal chain
                        chain += 1
                        ins.then_inc(tern_step, 1)
                        dve.wait_ge(tern_step, chain)

                    link(nc.vector.tensor_reduce(wsum[:, :], mxb[0][:, 0:2 * FT].rearrange("p (w f) -> p w f", w=2),
                                                 AX_X, ALU.add))
                    link(nc.vector.tensor_scalar(wscale[:, :], wsum[:, :], 1.0 / (D * FF), 1e-8, ALU.mult, ALU.max))
                    for i, sign in enumerate((0.5, -0.5)):
                        link(nc.vector.tensor_scalar(thr[:, i, :], wscale[:, :], sign, None, ALU.mult))
                    for w, w_s in ((0, W1_s), (1, W2_s)):
                        flat = w_s[:, :, :].rearrange("p k n -> p (k n)")
                        link(nc.vector.tensor_scalar(tneg[:, :], flat, thr[:, 1, w:w + 1], None, ALU.is_lt))
                        nc.vector.scalar_tensor_tensor(flat, flat, thr[:, 0, w:w + 1], tneg[:, :],
                                                       ALU.is_gt, ALU.subtract).then_inc(tern_set, 1)
                        dve.wait_ge(tern_set, w + 1)
                if b:
                    low_part(oT_lo, oT_hi, n, oT_hi_set, oT_lo_set)
                if first:
                    values()
                if a:
                    maxima(0)
                    maxima(1)
                if c:
                    mlp_out(0)
                if a:
                    maxima(2)
                    maxima(3)
                if c:
                    mlp_out(1)
                for s in range(SUB):
                    if a:
                        maxima(4 + s)
                    if b:
                        residual(s)
                if a:
                    max_parts()
                if b:
                    dve.wait_ge(x2_set, SUB * (n + 1))
                    statistics(1, n, x2)
                if b and batch is not None:
                    values()
                if c:
                    mlp_out(2)
                if b:
                    normalize(1, n, x2)
                if a:
                    dve.wait_ge(nmT_done, n + 2)
                    nc.vector.tensor_copy(nmT[:, :], turn[0][0:2 * HEADS, 0:BLK // 2].bitcast(BF16)).then_inc(nmT_set, 1)
                if c:
                    mlp_out(3)
            steps(dve, step)

        @block.tensor
        def _(pe):
            def transposes(src, src_set, blk, done):
                for h in range(KT):
                    for s in range(SUB):
                        if h == 0:
                            pe.wait_ge(src_set, SUB * blk + s + 1)
                        ins = nc.tensor.transpose(turn[h][:, s * P:(s + 1) * P], src[:, s, h * P:(h + 1) * P], ident[:, :])
                    ins.then_inc(done, 1)

            def three(out_, a_hi, a_lo, b_hi, b_lo, first, last):
                nc.tensor.matmul(out_, a_hi, b_hi, start=first, stop=False)
                nc.tensor.matmul(out_, a_lo, b_hi, start=False, stop=False)
                return nc.tensor.matmul(out_, a_hi, b_lo, start=False, stop=last)

            def step(n, par, a, b, c, own, batch):
                first, second = not b and not c, b and not c
                def scores(t0, t1):
                    for t in range(t0, t1):
                        h, i = divmod(t, TH)
                        rows = ROWS[i]
                        if t == 0:
                            pe.wait_ge(nmT_set, n + 1)
                        if t >= 2:
                            pe.wait_ge(exp_done, NT * n + t - 1)
                        elif c and batch is not None:
                            pe.wait_ge(wt_set, 4 * KT + 1)
                        cols = slice(i * P, i * P + rows)
                        o = ring[t % 2][:rows, :]
                        nc.tensor.matmul(o, K_hi[:, h, cols], qT_hi[:, h, :], start=True, stop=False)
                        nc.tensor.matmul(o, K_hi[:, h, cols], qT_lo[:, h, :], start=False, stop=False)
                        nc.tensor.matmul(o, K_lo[:, h, cols], qT_hi[:, h, :], start=False, stop=False)
                        nc.tensor.matmul(o, headsel[:, h, cols], nmT[:, :], start=False, stop=True).then_inc(s_done, 1)

                def query():
                    pe.wait_ge(xT_lo_set, KT * (n + 2))
                    if first:
                        pe.wait_ge(wq_lo_set, 1)
                    for h in range(KT):
                        cols = slice(h * P, (h + 1) * P)
                        for k in range(KT):
                            ins = three(turn[h][:, :], Wq_hi[:, k, cols], Wq_lo[:, k, cols], xT_hi[:, k, :], xT_lo[:, k, :],
                                        k == 0, k == KT - 1)
                        ins.then_inc(q_done, 1)

                def context_T():
                    pe.wait_ge(in_ctx, 16 * (batch + 1))
                    if b:
                        pe.wait_ge(q_lo_set, KT * (n + 2))
                    for k in range(KT):
                        ins = nc.tensor.transpose(turn[0][:, k * P:k * P + NK], ctx_s[:, k * P:(k + 1) * P],
                                                  ident[0:NK, 0:NK])
                    ins.then_inc(ctxT_done, 1)

                def keys():
                    pe.wait_ge(ctxT_set, KT * (batch + 1))
                    if first:
                        pe.wait_ge(in_wk, 16)
                    for h in range(KT):
                        for k in range(KT):
                            ins = nc.tensor.matmul(turn[1][:, h * P:h * P + NK], Wk_s[:, k, h * P:(h + 1) * P],
                                                   ctxT[:, k, 0:NK], start=(k == 0), stop=(k == KT - 1))
                    ins.then_inc(kT_done, 1)

                def values():
                    if first:
                        pe.wait_ge(in_wv, 16)
                        pe.wait_ge(q_lo_set, KT)
                    for t in range(TH):
                        if t >= 2:
                            pe.wait_ge(v_set, TH * batch + t - 1)
                        r = ROWS[t]
                        for k in range(KT):
                            ins = nc.tensor.matmul(turn[t % 2][:r, 0:D], ctxT[:, k, t * P:t * P + r], Wv_s[:, k, :],
                                                   start=(k == 0), stop=(k == KT - 1))
                        ins.then_inc(v_done, 1)

                def mlp_in(f0, f1):
                    for f in range(f0, f1):
                        if f == 0:
                            pe.wait_ge(x2T_lo_set, KT * n)
                        if f >= 2:
                            pe.wait_ge(gelu_done, FT * (n - 1) + f - 1)
                        elif b:
                            pe.wait_ge(exp_done, NT * (n + 1))
                        cols = slice(f * P, (f + 1) * P)
                        for k in range(KT):
                            for part in (x2T_hi, x2T_lo):
                                ins = nc.tensor.matmul(ring[f % 2][:, :], W1T[:, k, cols], part[:, k, :],
                                                       start=(k == 0 and part is x2T_hi),
                                                       stop=(k == KT - 1 and part is x2T_lo))
                        ins.then_inc(f1_done, 1)

                def attend(s):
                    if s == 0:
                        pe.wait_ge(exp_done, NT * (n + 1))
                        if second:
                            pe.wait_ge(v_ones_set, 2)
                        pe.wait_ge(v_set, TH * (own + 1))
                    if s:
                        pe.wait_ge(o_set, SUB * n + s)
                    for h in range(KT):
                        for i in range(TH):
                            r = ROWS[i]
                            ins = nc.tensor.matmul(o_ps[:, h * VC:(h + 1) * VC], probs[:r, h * TH + i, s * P:(s + 1) * P],
                                                   V_s[:r, i, h, :], start=(i == 0), stop=(i == TH - 1))
                    ins.then_inc(pv_done, 1)

                def max_scores(g):
                    s, h = divmod(g, KT)
                    if g == 0:
                        pe.wait_ge(q_lo_set, KT * (n + 2))
                        if first:
                            pe.wait_ge(k_lo_set, 1)
                    if first and g == 0:
                        pass
                    else:
                        pe.wait_ge(mx_red, NMX * (n + 1) + g)
                    if g == 0 and batch is not None:
                        pe.wait_ge(k_lo_set, batch + 1)
                    for i in range(2):
                        ins = nc.tensor.matmul(mxb[i][:, 0:HK // 2], qT_hi[:, h, s * P:(s + 1) * P],
                                               K_hi[:, h, i * (HK // 2):(i + 1) * (HK // 2)], start=True, stop=True)
                    ins.then_inc(mx_done, 1)

                def project(s):
                    if s == 0:
                        pe.wait_ge(oT_lo_set, KT * (n + 1))
                        if second:
                            pe.wait_ge(wo_lo_set, 1)
                    if s < 2:
                        if c:
                            pe.wait_ge(y_set, SUB * (n - 1) + s + 1)
                    else:
                        pe.wait_ge(x2_set, SUB * n + s - 1)
                    cols = slice(s * P, (s + 1) * P)
                    for k in range(KT):
                        o = ybank[s % 2][:, 0:D]
                        nc.tensor.matmul(o, oT_hi[:, k, cols], Wo_hi[:, k, :], start=(k == 0), stop=False)
                        nc.tensor.matmul(o, oT_lo[:, k, cols], Wo_hi[:, k, :], start=False, stop=False)
                        ins = nc.tensor.matmul(o, oT_hi[:, k, cols], Wo_lo[:, k, :], start=False, stop=(k == KT - 1))
                    ins.then_inc(wo_done, 1)

                def mlp_out(s):
                    if s == 0:
                        pe.wait_ge(h_lo_set, FT * n)
                    elif s == 1:
                        if b:
                            pe.wait_ge(o_set, SUB * (n + 1))
                    elif b:
                        pe.wait_ge(x2_set, SUB * n + s + 1)
                    else:
                        pe.wait_ge(y_set, SUB * (n - 1) + s - 1)
                    cols = slice(s * P, (s + 1) * P)
                    for f in range(FT):
                        for part in (h_hi, h_lo):
                            ins = nc.tensor.matmul(ybank[s % 2][:, 0:D], part[:, f, cols], W2T[:, f, :],
                                                   start=(f == 0 and part is h_hi), stop=(f == FT - 1 and part is h_lo))
                    ins.then_inc(f2_done, 1)

                def ternary_T():
                    pe.wait_ge(wabs_set, 2)
                    pe.wait_ge(ones_set, 1)
                    nc.tensor.matmul(mxb[0][:, 0:2 * FT], ones[:, :], wabs[:, :, :].rearrange("p w f -> p (w f)"),
                                     start=True, stop=True).then_inc(wsum_done, 1)
                    for g in range(4 * KT):
                        if g < 2:
                            pe.wait_ge(exp_done, NT)
                        else:
                            pe.wait_ge(wt_set, g - 1)
                        pe.wait_ge(tern_set, 1 if g < 2 * KT else 2)
                        for j in range(4):
                            if g < 2 * KT:
                                src = W1_s[:, g % 2 * 4 + j, g // 2 * P:(g // 2 + 1) * P]
                            else:
                                q = g - 2 * KT
                                ft = q % 2 * 4 + j
                                src = W2_s[:, q // 2, ft * P:(ft + 1) * P]
                            ins = nc.tensor.transpose(ring[g % 2][:, j * P:(j + 1) * P], src, ident[:, :])
                        ins.then_inc(wt_done, 1)
                    pe.wait_ge(in_b1, 16)
                    pe.wait_ge(wt_set, 4 * KT - 1)
                    nc.tensor.transpose(ring[0][:, 0:FT], b1_r[:, :], ident[0:FT, 0:FT]).then_inc(wt_done, 1)

                if first:
                    pe.wait_ge(pool_chain, 2)
                    context_T()
                    keys()
                    pe.wait_ge(k_masked, KT)
                if b:
                    scores(0, NT // 2)
                if c:
                    transposes(xn[1], xn_set[1], n - 1, x2T_done)
                if b:
                    scores(NT // 2, NT)
                if a:
                    if c:
                        pe.wait_ge(x2T_lo_set, KT * n)
                    transposes(xn[0], xn_set[0], n + 1, xT_done)
                if c:
                    mlp_in(0, 2)
                if b:
                    attend(0)
                if a:
                    query()
                if c:
                    mlp_in(2, 4)
                if b:
                    attend(1)
                if b and batch is not None:
                    context_T()
                if c:
                    mlp_in(4, 6)
                if b:
                    attend(2)
                if b and batch is not None:
                    keys()
                if c:
                    mlp_in(6, 8)
                if b:
                    attend(3)
                    if a:
                        pe.wait_ge(q_lo_set, KT * (n + 2))
                    if batch is not None:
                        pe.wait_ge(k_masked, KT * (batch + 1))
                if second:
                    ternary_T()
                if b:
                    transposes(o_s, o_set, n, oT_done)
                if first:
                    values()
                if a:
                    if second:
                        pe.wait_ge(tern_step, 1)
                    max_scores(0)
                    max_scores(1)
                if c:
                    mlp_out(0)
                if a:
                    max_scores(2)
                    max_scores(3)
                if c:
                    mlp_out(1)
                for s in range(SUB):
                    if a:
                        max_scores(4 + s)
                    if b:
                        project(s)
                if b and batch is not None:
                    values()
                if c:
                    mlp_out(2)
                if a:
                    pe.wait_ge(nm_set, n + 2)
                    if batch is not None:
                        pe.wait_ge(v_set, TH * (batch + 1))
                    if first:
                        pe.wait_ge(pool_chain, N_CONST)
                    for s in range(SUB):
                        ins = nc.tensor.transpose(turn[0][0:2 * HEADS, s * P // 2:(s + 1) * P // 2].bitcast(BF16),
                                                  nmb[:, s, :], ident_b[:, :])
                    ins.then_inc(nmT_done, 1)
                if c:
                    mlp_out(3)
            steps(pe, step)


_INS = ["x", "ctx_1024", "mask_B_ik0", "g_xattn", "g_ffn", "L0_xattn_Wq", "L0_xattn_Wk", "L0_xattn_Wv", "L0_xattn_Wo",
        "L0_ffn_W1", "L0_ffn_b1", "L0_ffn_W2", "L0_ffn_b2"]


def kernel(**inputs):
    import numpy as _np
    import concourse.bacc as _bacc
    from concourse import mybir as _mybir
    from concourse.bass_utils import run_bass_kernel_spmd as _run

    nc = _bacc.Bacc("TRN2", target_bir_lowering=False, num_devices=1)
    arrays, args = {}, []
    for name in _INS:
        if name == "mask_B_ik0":
            continue
        a = _np.ascontiguousarray(inputs[name])
        arrays[f"in_{name}_dram"] = a
        args.append(nc.dram_tensor(f"in_{name}_dram", a.shape, _mybir.dt.from_np(a.dtype), kind="ExternalInput").ap())
    shape = inputs["x"].shape
    args.append(nc.dram_tensor("out_dram", shape, _mybir.dt.float32, kind="ExternalOutput").ap())
    gated_cross_attention_block(nc, *args)
    r = _run(nc, [arrays], core_ids=[0])
    return r.results[0]["out_dram"]
```

```python
from contextlib import ExitStack

import concourse.bass as bass
from concourse import mybir

F32 = mybir.dt.float32
F32R = mybir.dt.float32r
BF16 = mybir.dt.bfloat16
F16 = mybir.dt.float16
ALU = mybir.AluOpType
ACT = mybir.ActivationFunctionType
AX_X = mybir.AxisListType.X

P = 128
HEADS = 16
EPS = 1e-5


def gated_cross_attention_block(nc, x, ctx, g_xattn, g_ffn, Wq, Wk, Wv, Wo, W1, b1, W2, b2, out):
    B, S, D = x.shape
    NK = ctx.shape[1]
    FF = W1.shape[0]
    DH = D // HEADS
    KT = D // P
    HH = P // DH
    FT = FF // P
    BLK = 512
    NB = B * S // BLK
    BPB = S // BLK
    SUB = BLK // P
    HK = HH * NK
    TH = -(-HK // P)
    NT = KT * TH
    ROWS = [min(P, HK - t * P) for t in range(TH)]
    VH = DH + 1
    HEADS_OF = [(t * P // NK, (t * P + ROWS[t] - 1) // NK + 1) for t in range(TH)]
    NMX = SUB * KT * 2
    MAX_AFTER = [[0, 0, 2], [2, 2, 2], [2, 2, 2], [1, 1, 0]]
    EARLY = FT - 2
    assert sum(map(sum, MAX_AFTER)) == NMX and FT == 2 * SUB
    assert BPB == 2 and NB >= 4 and HK % 2 == 0 and NT % 2 == 0 and FT % 2 == 0

    x_v = x.rearrange("b t d -> (b t) d").rearrange("(n p s) d -> n p (s d)", p=P, s=SUB)
    out_v = out.rearrange("b t d -> (b t) d").rearrange("(n p s) d -> n p (s d)", p=P, s=SUB)

    with ExitStack() as stack:
        def sb(name, shape, dt=F32):
            return stack.enter_context(nc.sbuf_tensor(name, shape, dt))

        def psum(name):
            return stack.enter_context(nc.psum_tensor(name, [P, 512], F32))

        def sem(name):
            return stack.enter_context(nc.semaphore(name))

        ring = [psum("ring0"), psum("ring1")]
        turn = [psum("turn0"), psum("turn1")]
        mxb = [psum("mxb0"), psum("mxb1")]
        o_ps = psum("o_ps")
        y_ps = psum("y_ps")
        ybank = [y_ps, o_ps]

        ident = sb("ident", [P, P])
        ident_b = sb("ident_b", [P, P], BF16)
        ones = sb("ones", [P, P])
        kmask = sb("kmask", [P, HH])
        vmask = sb("vmask", [P, TH, HH])
        headsel = sb("headsel", [2 * HEADS, KT, HK], BF16)
        keysel = sb("keysel", [NK, HK], F16)
        neg_half = sb("neg_half", [P, SUB])
        Wk_s = sb("Wk_s", [P, KT, D])
        Wv_s = sb("Wv_s", [P, KT, D])
        Wq_s = sb("Wq_s", [P, KT, D])
        Wo_s = sb("Wo_s", [P, KT, D])
        Wq_hi, Wq_lo = sb("Wq_hi", [P, KT, D], F32R), sb("Wq_lo", [P, KT, D], F32R)
        Wo_hi, Wo_lo = sb("Wo_hi", [P, KT, D], F32R), sb("Wo_lo", [P, KT, D], F32R)
        W1T = sb("W1T", [P, KT, FF], F32R)
        W2T = sb("W2T", [P, FT, D], F32R)
        b1_r = sb("b1_r", [FT, P])
        b1_s = sb("b1_s", [P, FT])
        b2_s = sb("b2_s", [P, D])
        b2_g = sb("b2_g", [P, D])
        gates = sb("gates", [P, 2])
        tg = sb("tg", [P, 2])
        wabs = sb("wabs", [P, 2, FT])
        wsum = sb("wsum", [P, 2])
        wscale = sb("wscale", [P, 2])
        thr = sb("thr", [P, 2, 2])

        ctx_s = sb("ctx_s", [NK, D])
        ctxT = sb("ctxT", [P, KT, NK])
        K_f = sb("K_f", [P, KT, HK])
        K_hi, K_lo = sb("K_hi", [P, KT, HK], F32R), sb("K_lo", [P, KT, HK], F32R)
        Vn = sb("Vn", [NK, 2, D], F16)
        V_s = sb("V_s", [P, TH, 2, KT, HH, VH], F16)

        xb = [sb(f"xb{i}", [P, SUB, D]) for i in range(2)]
        xr = sb("xr", [P, SUB, D])
        stats = [sb(f"stats{i}", [P, SUB, 6]) for i in range(2)]
        lnp = [sb(f"lnp{i}", [P, 6, SUB]) for i in range(2)]
        table = sb("table", [1, 4])
        rstd = [sb(f"rstd{i}", [P, SUB]) for i in range(2)]
        shift = [sb(f"shift{i}", [P, SUB]) for i in range(2)]
        xn = [sb(f"xn{i}", [P, SUB, D]) for i in range(2)]
        xT_hi, xT_lo = sb("xT_hi", [P, KT, BLK], F32R), sb("xT_lo", [P, KT, BLK], F32R)
        qT_hi, qT_lo = sb("qT_hi", [P, KT, BLK], F32R), sb("qT_lo", [P, KT, BLK], F32R)
        nm = sb("nm", [P, SUB, HEADS])
        nmb = sb("nmb", [P, SUB, 2 * HEADS], BF16)
        nmT = sb("nmT", [2 * HEADS, BLK], BF16)
        PR = NT // 2
        probs = sb("probs", [P, PR, BLK])
        p_hi, p_lo = sb("p_hi", [P, NT, BLK], F16), sb("p_lo", [P, NT, BLK], F16)
        rz = [sb(f"rz{i}", [P, HEADS]) for i in range(2)]
        o_s = sb("o_s", [P, SUB, D])
        oT_hi, oT_lo = xT_hi, xT_lo
        x2 = sb("x2", [P, SUB, D])
        x2T_hi, x2T_lo = sb("x2T_hi", [P, KT, BLK], F32R), sb("x2T_lo", [P, KT, BLK], F32R)
        h_f = sb("h_f", [P, FT, BLK])
        w12 = h_f[:, :, :].rearrange("p f n -> p (f n)")
        W1_s = w12[:, 0:FT * D].rearrange("p (f n) -> p f n", n=D)
        W2_s = w12[:, FT * D:].rearrange("p (k n) -> p k n", n=FF)
        h_hi, h_lo = sb("h_hi", [P, FT, BLK], F32R), sb("h_lo", [P, FT, BLK], F32R)
        y = [sb(f"y{i}", [P, SUB, D]) for i in range(2)]
        tneg = y[1][:, :, :].rearrange("p s d -> p (s d)")

        in_x = [sem(f"in_x{i}") for i in range(2)]
        in_r = sem("in_r")
        in_ctx = sem("in_ctx")
        in_wq, in_wk, in_wv, in_wo = sem("in_wq"), sem("in_wk"), sem("in_wv"), sem("in_wo")
        in_w1, in_w2, in_b1, in_b2, in_g = sem("in_w1"), sem("in_w2"), sem("in_b1"), sem("in_b2"), sem("in_g")
        pool_chain = sem("pool_chain")
        ones_set = sem("ones_set")
        tg_set, b2_set = sem("tg_set"), sem("b2_set")
        table_set = sem("table_set")
        wq_hi_set, wq_lo_set, wo_hi_set, wo_lo_set = (sem(f"{w}_set") for w in ("wq_hi", "wq_lo", "wo_hi", "wo_lo"))
        wabs_set, wsum_done, thr_step = sem("wabs_set"), sem("wsum_done"), sem("thr_step")
        tneg_set, tern_set = sem("tneg_set"), sem("tern_set")
        wt_done, wt_set = sem("wt_done"), sem("wt_set")
        ctxT_done, ctxT_set, kT_done, k_masked, k_hi_set, k_lo_set = (
            sem(s) for s in ("ctxT_done", "ctxT_set", "kT_done", "k_masked", "k_hi_set", "k_lo_set"))
        vn_done, vn_hi_set, vn_set = sem("vn_done"), sem("vn_hi_set"), sem("vn_set")
        v_done, v_set, v_ones_set = sem("v_done"), sem("v_set"), sem("v_ones_set")
        st_set, half_set, mean_set, sq_set, var_set, ve_set, rstd_set, shift_set, xn_set = (
            [sem(f"{s}{i}") for i in range(2)]
            for s in ("st_set", "half_set", "mean_set", "sq_set", "var_set", "ve_set", "rstd_set", "shift_set", "xn_set"))
        xT_done, xT_hi_set, xT_lo_set = sem("xT_done"), sem("xT_hi_set"), sem("xT_lo_set")
        q_done, q_hi_set, q_lo_set = sem("q_done"), sem("q_hi_set"), sem("q_lo_set")
        mx_done, mx_red, nm_hi_set, nm_set = sem("mx_done"), sem("mx_red"), sem("nm_hi_set"), sem("nm_set")
        nmT_done, nmT_set = sem("nmT_done"), sem("nmT_set")
        s_done, exp_done, p_hi_set, p_lo_set, pv_done, rz_set, o_set = (
            sem(s) for s in ("s_done", "exp_done", "p_hi_set", "p_lo_set", "pv_done", "rz_set", "o_set"))
        oT_done, oT_hi_set, oT_lo_set = sem("oT_done"), sem("oT_hi_set"), sem("oT_lo_set")
        wo_done, x2_set, y_base = sem("wo_done"), sem("x2_set"), sem("y_base")
        x2T_done, x2T_hi_set, x2T_lo_set = sem("x2T_done"), sem("x2T_hi_set"), sem("x2T_lo_set")
        f1_done, gelu_done, h_hi_set, h_lo_set, h_last_hi_set, h_last_lo_set, f2_done, y_set = (
            sem(s) for s in ("f1_done", "gelu_done", "h_hi_set", "h_lo_set", "h_last_hi_set", "h_last_lo_set",
                             "f2_done", "y_set"))
        y_free = [sem(f"y_free{i}") for i in range(2)]

        N_CONST = 15

        def steps(eng, step):
            step(-1, 1, True, False, False, None, 0)
            step(0, 0, True, True, False, 0, None)
            with eng.Fori(0, (NB - 2) // 2) as i:
                step(2 * i + 1, 1, True, True, True, i, i + 1)
                step(2 * i + 2, 0, True, True, True, i + 1, None)
            step(NB - 1, 1, False, True, True, NB // BPB - 1, None)
            step(NB, 0, False, False, True, None, None)

        block = stack.enter_context(nc.Block())

        @block.sync
        def _(sp):
            sp.dma_start(xb[0][:, :, :], x_v[0].rearrange("p (s d) -> p s d", s=SUB)).then_inc(in_x[0], 16)
            sp.dma_start(ctx_s[:, :], ctx[0]).then_inc(in_ctx, 16)
            for w, w_s, w_in in ((Wq, Wq_s, in_wq), (Wk, Wk_s, in_wk), (Wv, Wv_s, in_wv), (Wo, Wo_s, in_wo)):
                sp.dma_start(w_s[:, :, :], w.rearrange("(k p) n -> p k n", p=P)).then_inc(w_in, 16)
            sp.dma_start(gates[:, 0:1], g_xattn.partition_broadcast(P)).then_inc(in_g, 16)
            sp.dma_start(gates[:, 1:2], g_ffn.partition_broadcast(P)).then_inc(in_g, 16)
            sp.dma_start(b2_s[:, :], b2.partition_broadcast(P)).then_inc(in_b2, 16)
            sp.dma_start(b1_r[:, :], b1.rearrange("(f p) -> f p", p=P)).then_inc(in_b1, 16)
            sp.dma_start(xb[1][:, :, :], x_v[1].rearrange("p (s d) -> p s d", s=SUB)).then_inc(in_x[1], 16)
            sp.dma_start(W1_s[:, :, :], W1.rearrange("(f p) n -> p f n", p=P)).then_inc(in_w1, 16)
            sp.dma_start(W2_s[:, :, :], W2.rearrange("(k p) n -> p k n", p=P)).then_inc(in_w2, 16)

            def step(n, par, a, b, c, own, batch):
                first, second = not b and not c, b and not c
                prep_v = b and par == 0
                if b and a and c:
                    sp.wait_ge(xn_set[0], SUB * n)
                    sp.dma_start(xb[1 - par][:, :, :], x_v[n + 1].rearrange("p (s d) -> p s d", s=SUB)
                                 ).then_inc(in_x[1 - par], 16)
                if b and batch is not None:
                    sp.wait_ge(ctxT_done, batch)
                    sp.dma_start(ctx_s[:, :], ctx[batch]).then_inc(in_ctx, 16)
                if b and c:
                    sp.wait_ge(x2_set, SUB * n)
                if b:
                    sp.dma_start(xr[:, :, :], x_v[n].rearrange("p (s d) -> p s d", s=SUB)).then_inc(in_r, 16)
            steps(sp, step)
            for par in range(2):
                sp.wait_ge(y_free[par], 16 * (NB // 2 + 1))

        @block.gpsimd
        def _(pool):
            done = [0]

            def chain(ins):
                done[0] += 1
                ins.then_inc(pool_chain, 1)
                return done[0]

            def band(t, pattern, width):
                pool.wait_ge(pool_chain, chain(nc.gpsimd.affine_select(
                    out=t, in_=t, pattern=[[-s, c] for s, c in pattern], compare_op=ALU.is_ge, fill=0.0,
                    base=0, channel_multiplier=1)))
                return chain(nc.gpsimd.affine_select(
                    out=t, in_=t, pattern=pattern, compare_op=ALU.is_ge, fill=0.0,
                    base=width - 1, channel_multiplier=-1))

            def diagonal(t, pattern, base):
                return chain(nc.gpsimd.affine_select(
                    out=t, in_=t, pattern=pattern, compare_op=ALU.not_equal, fill=1.0,
                    base=base, channel_multiplier=-1))

            pool.wait_ge(pool_chain, chain(nc.gpsimd.memset(ident[:, :], 0.0)))
            diagonal(ident[:, :], [[1, P]], 0)
            chain(nc.gpsimd.memset(neg_half[:, :], -0.5))
            for i in range(2):
                nc.gpsimd.memset(y[i][:, 0, 0:1], 0.0).then_inc(y_free[i], 16)
            pool.wait_ge(pool_chain, chain(nc.gpsimd.memset(kmask[:, :], 1.0)))
            band(kmask[:, :], [[DH, HH]], DH)

            def inverse_deviation(which, blk):
                pool.wait_ge(ve_set[which], blk + 1)
                nc.gpsimd.tensor_tensor(rstd[which][:, :], lnp[which][:, 5, :], neg_half[:, :], ALU.pow
                                        ).then_inc(rstd_set[which], 1)
                pool.wait_ge(mean_set[which], blk + 1)
                pool.wait_ge(rstd_set[which], blk + 1)
                nc.gpsimd.tensor_tensor(shift[which][:, :], lnp[which][:, 3, :], rstd[which][:, :], ALU.mult
                                        ).then_inc(shift_set[which], 1)

            def prepare():
                pool.wait_ge(in_wq, 16)
                pool.wait_ge(wq_hi_set, 1)
                nc.gpsimd.tensor_tensor(Wq_lo[:, :, :], Wq_s[:, :, :], Wq_hi[:, :, :].bitcast(F32), ALU.subtract
                                        ).then_inc(wq_lo_set, 1)
                pool.wait_ge(pool_chain, chain(nc.gpsimd.memset(vmask[:, :, :], 1.0)))
                pool.wait_ge(pool_chain, chain(nc.gpsimd.affine_select(
                    out=vmask[:, :, :], in_=vmask[:, :, :], pattern=[[P, TH], [-NK, HH]], compare_op=ALU.is_ge,
                    fill=0.0, base=0, channel_multiplier=1)))
                chain(nc.gpsimd.affine_select(
                    out=vmask[:, :, :], in_=vmask[:, :, :], pattern=[[-P, TH], [NK, HH]], compare_op=ALU.is_ge,
                    fill=0.0, base=NK - 1, channel_multiplier=-1))
                sel = headsel[:, :, :].rearrange("r k (h m) -> r k h m", h=HH)
                pool.wait_ge(pool_chain, chain(nc.gpsimd.memset(sel, 0.0)))
                pool.wait_ge(pool_chain, diagonal(sel, [[HH, KT], [1, HH], [0, NK]], 0))
                diagonal(sel, [[HH, KT], [1, HH], [0, NK]], HEADS)
                chain(nc.gpsimd.tensor_copy(ident_b[:, :], ident[:, :]))
                by_key = keysel[:, :].rearrange("r (h m) -> r h m", h=HH)
                pool.wait_ge(pool_chain, chain(nc.gpsimd.memset(by_key, 0.0)))
                diagonal(by_key, [[0, HH], [1, NK]], 0)
                assert done[0] == N_CONST, done
                pool.wait_ge(wo_hi_set, 1)
                nc.gpsimd.tensor_tensor(Wo_lo[:, :, :], Wo_s[:, :, :], Wo_hi[:, :, :].bitcast(F32), ALU.subtract
                                        ).then_inc(wo_lo_set, 1)
                pool.wait_ge(in_b2, 16)
                pool.wait_ge(tg_set, 1)
                nc.gpsimd.tensor_scalar(b2_g[:, :], b2_s[:, :], tg[:, 1:2], None, ALU.mult).then_inc(b2_set, 1)

            def step(n, par, a, b, c, own, batch):
                first, second = not b and not c, b and not c
                prep_v = b and par == 0
                if first:
                    pool.wait_ge(pool_chain, 3)
                    inverse_deviation(0, n + 1)
                if first:
                    prepare()
                if b:
                    for t in range(NT):
                        pool.wait_ge(p_hi_set, NT * n + t + 1)
                        rows = ROWS[t % TH]
                        nc.gpsimd.tensor_tensor(p_lo[:rows, t, :], probs[:rows, t % PR, :], p_hi[:rows, t, :], ALU.subtract
                                                ).then_inc(p_lo_set, 1)
                        if t == 0 and a:
                            inverse_deviation(0, n + 1)
                if c:
                    for f in range(EARLY):
                        pool.wait_ge(h_hi_set, (FT - 1) * (n - 1) + f + 1)
                        nc.gpsimd.tensor_tensor(h_lo[:, f, :], h_f[:, f, :], h_hi[:, f, :].bitcast(F32), ALU.subtract
                                                ).then_inc(h_lo_set, 1)
                if b:
                    inverse_deviation(1, n)
                    if second:
                        pool.wait_ge(b2_set, 1)
                    if c:
                        pool.wait_ge(y_free[par], 16 * (own + 1))
                    nc.gpsimd.tensor_tensor(y[par][:, :, :], x2[:, :, :],
                                            b2_g[:, :].unsqueeze(1).broadcast_to([P, SUB, D]), ALU.add
                                            ).then_inc(y_base, 1)
            steps(pool, step)

        @block.scalar
        def _(act):
            def copy(dst, src, done):
                nc.scalar.activation(dst, src, ACT.Copy).then_inc(done, 1)

            def normalize(which, blk, src, transposed):
                act.wait_ge(shift_set[which], blk + 1)
                if transposed:
                    act.wait_ge(transposed, KT * blk)
                for s in range(SUB):
                    nc.scalar.activation(xn[which][:, s, :], src[:, s, :], ACT.Identity, bias=shift[which][:, s:s + 1],
                                         scale=rstd[which][:, s:s + 1]).then_inc(xn_set[which], 1)

            def fetch_table(func, fetched):
                act.wait_ge(table_set, fetched + 1)
                nc.scalar.activation(table[:, 1:2], table[:, 0:1], func).then_inc(table_set, 1)

            act.wait_ge(in_wq, 16)
            copy(Wq_hi[:, :, :], Wq_s[:, :, :], wq_hi_set)
            act.wait_ge(in_g, 32)
            nc.scalar.activation(tg[:, :], gates[:, :], ACT.Tanh).then_inc(tg_set, 1)

            def step(n, par, a, b, c, own, batch):
                first, second = not b and not c, b and not c
                prep_v = b and par == 0
                def scores(t0, t1):
                    for t in range(t0, t1):
                        rows = ROWS[t % TH]
                        act.wait_ge(s_done, NT * n + t + 1)
                        if c or t >= PR:
                            act.wait_ge(p_lo_set, NT * n + t - PR + 1)
                        nc.scalar.activation(probs[:rows, t % PR, :], ring[t % 2][:rows, :], ACT.Exp
                                             ).then_inc(exp_done, 1)

                def high_part(dst, bank, blk, done, hi_set, h):
                    act.wait_ge(done, KT * blk + h + 1)
                    copy(dst[:, h, :], bank[h][:, :], hi_set)

                def gelu(f):
                    act.wait_ge(f1_done, FT * (n - 1) + f + 1)
                    nc.scalar.activation(h_f[:, f, :], ring[f % 2][:, :], ACT.Gelu, bias=b1_s[:, f:f + 1]
                                         ).then_inc(gelu_done, 1)

                def h_high(f):
                    act.wait_ge(gelu_done, FT * (n - 1) + f + 1)
                    copy(h_hi[:, f, :], h_f[:, f, :], h_hi_set)

                if b:
                    scores(0, 2)
                if c:
                    high_part(x2T_hi, mxb, n - 1, x2T_done, x2T_hi_set, 0)
                if b:
                    scores(2, 3)
                if c:
                    high_part(x2T_hi, mxb, n - 1, x2T_done, x2T_hi_set, 1)
                if b:
                    scores(3, 4)
                if a:
                    normalize(0, n + 1, xb[1 - par], None if first else xT_done)
                if b:
                    scores(4, 6)
                if a:
                    if c:
                        act.wait_ge(wo_done, SUB * n)
                    high_part(xT_hi, turn, n + 1, xT_done, xT_hi_set, 0)
                if b:
                    scores(6, 7)
                if a:
                    high_part(xT_hi, turn, n + 1, xT_done, xT_hi_set, 1)
                if b:
                    scores(7, NT)
                if c:
                    fetch_table(ACT.Gelu, 2 * n - 2)
                if a:
                    for h in range(KT):
                        if b and h == 0:
                            act.wait_ge(mx_done, NMX * (n + 1))
                        high_part(qT_hi, turn, n + 1, q_done, q_hi_set, h)
                if first:
                    act.wait_ge(in_wo, 16)
                    copy(Wo_hi[:, :, :], Wo_s[:, :, :], wo_hi_set)
                if c:
                    gelu(0)
                    for f in range(1, FT):
                        gelu(f)
                        h_high(f - 1)
                    if b:
                        fetch_table(ACT.Exp, 2 * n - 1)
                if b:
                    if a:
                        act.wait_ge(q_done, KT * (n + 2))
                    for h in range(KT):
                        high_part(oT_hi, turn, n, oT_done, oT_hi_set, h)
                    normalize(1, n, x2, x2T_done if c else None)
                if c:
                    act.wait_ge(y_set, SUB * n)
                    act.dma_start(out_v[n - 1].rearrange("p (s d) -> p s d", s=SUB), y[1 - par][:, :, :]
                                  ).then_inc(y_free[1 - par], 16)
                if second:
                    for g in range(4 * KT):
                        act.wait_ge(wt_done, g + 1)
                        dst = W1T[:, g // 2 % KT, g % 2 * 512:g % 2 * 512 + 512] if g < 2 * KT else (
                            W2T[:, :, :].rearrange("p (q f) (k d) -> p k q f d", q=2, k=KT)[:, (g - 2 * KT) // 2, g % 2])
                        src = ring[g % 2][:, :]
                        if g >= 2 * KT:
                            src = src.rearrange("p (f d) -> p f d", d=P)
                        copy(dst, src, wt_set)
                    act.wait_ge(wt_done, 4 * KT + 1)
                    copy(b1_s[:, :], ring[0][:, 0:FT], wt_set)
            steps(act, step)

        @block.vector
        def _(dve):
            def subtile_statistics(which, s, src):
                nc.vector.bn_stats(stats[which][:, s, :], src[:, s, :]).then_inc(st_set[which], 1)

            def statistics(which, blk):
                diff, total, m2, minus_mean, sq, ve = (lnp[which][:, i, :] for i in range(6))
                dve.wait_ge(st_set[which], SUB * (blk + 1))
                even, odd = stats[which][:, :, 0:3], stats[which][:, :, 3:6]
                nc.vector.tensor_tensor(diff, even[:, :, 1], odd[:, :, 1], ALU.subtract).then_inc(half_set[which], 1)
                nc.vector.tensor_tensor(total, even[:, :, 1], odd[:, :, 1], ALU.add).then_inc(half_set[which], 1)
                nc.vector.tensor_tensor(m2, even[:, :, 2], odd[:, :, 2], ALU.add).then_inc(half_set[which], 1)
                dve.wait_ge(half_set[which], 3 * (blk + 1))
                nc.vector.scalar_tensor_tensor(sq, diff, D / 4, diff, ALU.mult, ALU.mult).then_inc(sq_set[which], 1)
                nc.vector.tensor_scalar(minus_mean, total, -0.5, None, ALU.mult).then_inc(mean_set[which], 1)
                dve.wait_ge(sq_set[which], blk + 1)
                nc.vector.tensor_tensor(diff, sq, m2, ALU.add).then_inc(var_set[which], 1)
                dve.wait_ge(var_set[which], blk + 1)
                nc.vector.tensor_scalar(ve, diff, 1.0 / D, EPS, ALU.mult, ALU.add).then_inc(ve_set[which], 1)

            def low_part(dst, hi, bank, blk, hi_set, lo_set, h):
                dve.wait_ge(hi_set, KT * blk + h + 1)
                nc.vector.tensor_tensor(dst[:, h, :], bank[h][:, :], hi[:, h, :].bitcast(F32), ALU.subtract
                                        ).then_inc(lo_set, 1)

            nc.vector.memset(table[:, :], 0.0).then_inc(table_set, 1)
            nc.vector.memset(ones[:, :], 1.0).then_inc(ones_set, 1)
            nc.vector.memset(V_s[:, :, :, :, :, :].rearrange("p t w k h c -> p (t w k h c)"), 0.0).then_inc(v_ones_set, 1)

            def step(n, par, a, b, c, own, batch):
                first, second = not b and not c, b and not c
                prep_v = b and par == 0
                def context_T():
                    dve.wait_ge(ctxT_done, batch + 1)
                    if b:
                        dve.wait_ge(vn_done, batch)
                    nc.vector.tensor_copy(ctxT[:, :, :], mxb[0][:, 0:KT * P].rearrange("p (k c) -> p k c", k=KT)[:, :, 0:NK]
                                          ).then_inc(ctxT_set, 1)

                def keys():
                    dve.wait_ge(kT_done, batch + 1)
                    if first:
                        dve.wait_ge(pool_chain, 6)
                    for k in range(KT):
                        src = mxb[1][:, k * P:k * P + NK].unsqueeze(1).broadcast_to([P, HH, NK])
                        msk = kmask[:, :].unsqueeze(2).broadcast_to([P, HH, NK])
                        nc.vector.tensor_tensor(K_f[:, k, :].rearrange("p (h m) -> p h m", h=HH), src, msk, ALU.mult
                                                ).then_inc(k_masked, 1)

                def keys_high():
                    if b:
                        dve.wait_ge(s_done, NT * (n + 1))
                    dve.wait_ge(k_masked, KT * (batch + 1))
                    nc.vector.tensor_copy(K_hi[:, :, :], K_f[:, :, :]).then_inc(k_hi_set, 1)

                def keys_low():
                    dve.wait_ge(k_hi_set, batch + 1)
                    nc.vector.tensor_tensor(K_lo[:, :, :], K_f[:, :, :], K_hi[:, :, :].bitcast(F32), ALU.subtract
                                            ).then_inc(k_lo_set, 1)

                def values():
                    dve.wait_ge(vn_done, own + 1)
                    if c:
                        dve.wait_ge(v_done, TH * own)
                    nc.vector.tensor_copy(Vn[:, 0, :], y_ps[0:NK, 0:D]).then_inc(vn_hi_set, 1)
                    dve.wait_ge(vn_hi_set, own + 1)
                    nc.vector.tensor_tensor(Vn[:, 1, :], y_ps[0:NK, 0:D], Vn[:, 0, :], ALU.subtract
                                            ).then_inc(vn_set, 1)

                def value_rows(t0, t1):
                    for t in range(t0, t1):
                        dve.wait_ge(v_done, TH * own + t + 1)
                        if c and t == 0:
                            dve.wait_ge(pv_done, SUB * n)
                        if second and t == 0:
                            dve.wait_ge(pool_chain, N_CONST)
                            dve.wait_ge(v_ones_set, 1)
                        r = ROWS[t]
                        dst = V_s[:r, t].rearrange("p w k h c -> p (w k) h c")[:, :, :, 0:DH]
                        src = ybank[(t + 1) % 2][:r, :].rearrange("p (w h d) -> p w h d", w=2 * KT, h=HH)
                        msk = vmask[:r, t, :].unsqueeze(1).unsqueeze(3).broadcast_to([r, 2 * KT, HH, DH])
                        nc.vector.tensor_tensor(dst, src, msk, ALU.mult).then_inc(v_set, 1)
                        if second:
                            nc.vector.tensor_copy(V_s[:, t, 0, :, :, DH], vmask[:, t, :].unsqueeze(1).broadcast_to([P, KT, HH])
                                                  ).then_inc(v_ones_set, 1)

                def p_high(t):
                    rows = ROWS[t % TH]
                    dve.wait_ge(exp_done, NT * n + t + 1)
                    if t == 0 and c:
                        dve.wait_ge(pv_done, SUB * n)
                    nc.vector.tensor_copy(p_hi[:rows, t, :], probs[:rows, t % PR, :]).then_inc(p_hi_set, 1)

                def h_low(f):
                    if f == FT - 1:
                        dve.wait_ge(gelu_done, FT * n)
                        nc.vector.tensor_copy(h_hi[:, f, :], h_f[:, f, :]).then_inc(h_last_hi_set, 1)
                        dve.wait_ge(h_last_hi_set, n)
                    else:
                        dve.wait_ge(h_hi_set, (FT - 1) * (n - 1) + f + 1)
                    nc.vector.tensor_tensor(h_lo[:, f, :], h_f[:, f, :], h_hi[:, f, :].bitcast(F32), ALU.subtract
                                            ).then_inc(h_last_lo_set, 1)

                def head_outputs(s):
                    dve.wait_ge(pv_done, SUB * n + s + 1)
                    o_v = o_ps[:, 0:HEADS * VH].rearrange("p (h c) -> p h c", c=VH)
                    nc.vector.reciprocal(rz[s % 2][:, :], o_v[:, :, DH]).then_inc(rz_set, 1)
                    dve.wait_ge(rz_set, SUB * n + s + 1)
                    nc.vector.tensor_tensor(
                        o_s[:, s, :].rearrange("p (h d) -> p h d", h=HEADS), o_v[:, :, 0:DH],
                        rz[s % 2][:, :].unsqueeze(2).broadcast_to([P, HEADS, DH]), ALU.mult).then_inc(o_set, 1)

                def maxima(g):
                    s, hh = divmod(g, 2 * KT)
                    dve.wait_ge(mx_done, NMX * (n + 1) + g + 1)
                    nc.vector.tensor_reduce(nm[:, s, hh * (HH // 2):(hh + 1) * (HH // 2)],
                                            mxb[g % 2][:, 0:HK // 2].rearrange("p (h m) -> p h m", m=NK), AX_X, ALU.max,
                                            negate=True).then_inc(mx_red, 1)

                def max_parts():
                    dve.wait_ge(mx_red, NMX * (n + 2))
                    nc.vector.tensor_copy(nmb[:, :, 0:HEADS], nm[:, :, :]).then_inc(nm_hi_set, 1)
                    dve.wait_ge(nm_hi_set, n + 2)
                    nc.vector.tensor_tensor(nmb[:, :, HEADS:], nm[:, :, :], nmb[:, :, 0:HEADS], ALU.subtract
                                            ).then_inc(nm_set, 1)

                def residual(s):
                    dve.wait_ge(wo_done, SUB * n + s + 1)
                    if s == 0:
                        dve.wait_ge(in_r, 16 * (n + 1))
                    if c and s == 0:
                        dve.wait_ge(xn_set[1], SUB * n)
                        dve.wait_ge(y_base, n)
                    nc.vector.scalar_tensor_tensor(x2[:, s, :], ybank[s % 2][:, 0:D], tg[:, 0:1], xr[:, s, :],
                                                   ALU.mult, ALU.add).then_inc(x2_set, 1)

                def mlp_out(s):
                    dve.wait_ge(f2_done, SUB * (n - 1) + s + 1)
                    dve.wait_ge(y_base, n)
                    yv = y[1 - par][:, s, :]
                    nc.vector.scalar_tensor_tensor(yv, ybank[s % 2][:, 0:D], tg[:, 1:2], yv, ALU.mult, ALU.add
                                                   ).then_inc(y_set, 1)

                def weight_sizes():
                    dve.wait_ge(in_w1, 16)
                    nc.vector.tensor_reduce(wabs[:, 0, :], W1_s[:, :, :], AX_X, ALU.add,
                                            apply_absolute_value=True).then_inc(wabs_set, 1)
                    dve.wait_ge(in_w2, 16)
                    nc.vector.tensor_reduce(wabs[:, 1, :], W2_s[:, :, :].rearrange("p k (c d) -> p (k c) d", d=D),
                                            AX_X, ALU.add, apply_absolute_value=True).then_inc(wabs_set, 1)

                def thresholds():
                    dve.wait_ge(wsum_done, 1)
                    nc.vector.tensor_reduce(wsum[:, :], y_ps[:, 0:2 * FT].rearrange("p (w f) -> p w f", w=2),
                                            AX_X, ALU.add).then_inc(thr_step, 1)
                    dve.wait_ge(thr_step, 1)
                    nc.vector.tensor_scalar(wscale[:, :], wsum[:, :], 1.0 / (D * FF), 1e-8, ALU.mult, ALU.max
                                            ).then_inc(thr_step, 1)
                    dve.wait_ge(thr_step, 2)
                    for i, sign in enumerate((0.5, -0.5)):
                        nc.vector.tensor_scalar(thr[:, i, :], wscale[:, :], sign, None, ALU.mult).then_inc(thr_step, 1)
                    dve.wait_ge(thr_step, 4)

                def ternary(w, w_s):
                    flat = w_s[:, :, :].rearrange("p k n -> p (k n)")
                    half = FT * D // 2
                    for i in range(2):
                        part = flat[:, i * half:(i + 1) * half]
                        if w or i:
                            dve.wait_ge(tern_set, 2 * w + i)
                        nc.vector.tensor_scalar(tneg, part, thr[:, 1, w:w + 1], None, ALU.is_lt).then_inc(tneg_set, 1)
                        dve.wait_ge(tneg_set, 2 * w + i + 1)
                        nc.vector.scalar_tensor_tensor(part, part, thr[:, 0, w:w + 1], tneg,
                                                       ALU.is_gt, ALU.subtract).then_inc(tern_set, 1)

                def split(t0, t1):
                    if b:
                        for t in range(t0, t1):
                            p_high(t)

                if a:
                    dve.wait_ge(in_x[1 - par], 16 * ((own if batch is None else batch) + 1))
                    for s in range(SUB):
                        subtile_statistics(0, s, xb[1 - par])
                    statistics(0, n + 1)
                split(0, 2)
                if c:
                    low_part(x2T_lo, x2T_hi, mxb, n - 1, x2T_hi_set, x2T_lo_set, 0)
                if c:
                    low_part(x2T_lo, x2T_hi, mxb, n - 1, x2T_hi_set, x2T_lo_set, 1)
                split(2, 4)
                if batch is not None:
                    context_T()
                if prep_v:
                    values()
                split(4, 6)
                if a:
                    low_part(xT_lo, xT_hi, turn, n + 1, xT_hi_set, xT_lo_set, 0)
                if prep_v:
                    value_rows(0, 2)
                if a:
                    low_part(xT_lo, xT_hi, turn, n + 1, xT_hi_set, xT_lo_set, 1)
                split(6, 7)
                if batch is not None:
                    keys()
                if prep_v:
                    value_rows(2, 3)
                split(7, 8)
                if prep_v:
                    value_rows(3, 4)
                split(8, 9)
                if prep_v:
                    value_rows(4, TH)
                split(9, NT)
                if a:
                    for h in range(KT):
                        low_part(qT_lo, qT_hi, turn, n + 1, q_hi_set, q_lo_set, h)
                if batch is not None:
                    keys_high()
                if second:
                    thresholds()
                    ternary(0, W1_s)
                if a or b:
                    g = 0
                    for r in range(SUB):
                        for i in range(2):
                            if a:
                                for _ in range(MAX_AFTER[r][i]):
                                    maxima(g)
                                    g += 1
                        if a:
                            for _ in range(MAX_AFTER[r][2]):
                                maxima(g)
                                g += 1
                        if c and r == SUB - 1:
                            for f in range(EARLY, FT):
                                h_low(f)
                        if b:
                            head_outputs(r)
                else:
                    for f in range(EARLY, FT):
                        h_low(f)
                if a:
                    max_parts()
                if batch is not None:
                    keys_low()
                if c:
                    mlp_out(0)
                if b:
                    for h in range(KT):
                        low_part(oT_lo, oT_hi, turn, n, oT_hi_set, oT_lo_set, h)
                if a:
                    dve.wait_ge(nmT_done, n + 2)
                    nc.vector.tensor_copy(nmT[:, :], mxb[0][0:2 * HEADS, 0:BLK // 2].bitcast(BF16)).then_inc(nmT_set, 1)
                if c:
                    mlp_out(1)
                if b:
                    for s in range(SUB + 1):
                        if s < SUB:
                            residual(s)
                        if s:
                            dve.wait_ge(x2_set, SUB * n + s)
                            subtile_statistics(1, s - 1, x2)
                    statistics(1, n)
                if c:
                    mlp_out(2)
                if c:
                    mlp_out(3)
                if first:
                    weight_sizes()
                if second:
                    ternary(1, W2_s)
            steps(dve, step)

        @block.tensor
        def _(pe):
            def transposes(src, src_set, bank, blk, done):
                for h in range(KT):
                    for s in range(SUB):
                        if h == 0:
                            pe.wait_ge(src_set, SUB * blk + s + 1)
                        ins = nc.tensor.transpose(bank[h][:, s * P:(s + 1) * P], src[:, s, h * P:(h + 1) * P], ident[:, :])
                    ins.then_inc(done, 1)

            def three(out_, a_hi, a_lo, b_hi, b_lo, first, last):
                nc.tensor.matmul(out_, a_hi, b_hi, start=first, stop=False)
                nc.tensor.matmul(out_, a_lo, b_hi, start=False, stop=False)
                return nc.tensor.matmul(out_, a_hi, b_lo, start=False, stop=last)

            def step(n, par, a, b, c, own, batch):
                first, second = not b and not c, b and not c
                prep_v = b and par == 0
                def scores(t0, t1):
                    for t in range(t0, t1):
                        h, i = divmod(t, TH)
                        rows = ROWS[i]
                        if t == 0:
                            pe.wait_ge(nmT_set, n + 1)
                            pe.wait_ge(k_lo_set, own + 1)
                            pe.wait_ge(q_lo_set, KT * (n + 1))
                        if t >= 2:
                            pe.wait_ge(exp_done, NT * n + t - 1)
                        elif c and batch is not None:
                            pe.wait_ge(wt_set, 4 * KT + 1)
                        cols = slice(i * P, i * P + rows)
                        o = ring[t % 2][:rows, :]
                        nc.tensor.matmul(o, K_hi[:, h, cols], qT_hi[:, h, :], start=True, stop=False)
                        nc.tensor.matmul(o, K_hi[:, h, cols], qT_lo[:, h, :], start=False, stop=False)
                        nc.tensor.matmul(o, K_lo[:, h, cols], qT_hi[:, h, :], start=False, stop=False)
                        nc.tensor.matmul(o, headsel[:, h, cols], nmT[:, :], start=False, stop=True).then_inc(s_done, 1)

                def query():
                    pe.wait_ge(xT_lo_set, KT * (n + 2))
                    if first:
                        pe.wait_ge(wq_lo_set, 1)
                    for h in range(KT):
                        cols = slice(h * P, (h + 1) * P)
                        for k in range(KT):
                            ins = three(turn[h][:, :], Wq_hi[:, k, cols], Wq_lo[:, k, cols], xT_hi[:, k, :], xT_lo[:, k, :],
                                        k == 0, k == KT - 1)
                        ins.then_inc(q_done, 1)

                def context_T():
                    pe.wait_ge(in_ctx, 16 * (batch + 1))
                    if c:
                        pe.wait_ge(x2T_lo_set, KT * n)
                    for k in range(KT):
                        ins = nc.tensor.transpose(mxb[0][:, k * P:k * P + NK], ctx_s[:, k * P:(k + 1) * P],
                                                  ident[0:NK, 0:NK])
                    ins.then_inc(ctxT_done, 1)

                def keys():
                    pe.wait_ge(ctxT_set, batch + 1)
                    if first:
                        pe.wait_ge(in_wk, 16)
                    for h in range(KT):
                        for k in range(KT):
                            ins = nc.tensor.matmul(mxb[1][:, h * P:h * P + NK], Wk_s[:, k, h * P:(h + 1) * P],
                                                   ctxT[:, k, 0:NK], start=(k == 0), stop=(k == KT - 1))
                    ins.then_inc(kT_done, 1)

                def values():
                    if second:
                        pe.wait_ge(in_wv, 16)
                    if c:
                        pe.wait_ge(y_set, SUB * (n - 1))
                    for k in range(KT):
                        ins = nc.tensor.matmul(y_ps[0:NK, 0:D], ctxT[:, k, :], Wv_s[:, k, :],
                                               start=(k == 0), stop=(k == KT - 1))
                    ins.then_inc(vn_done, 1)

                def value_rows(t0, t1):
                    if t0 == 0:
                        pe.wait_ge(vn_set, own + 1)
                        if second:
                            pe.wait_ge(pool_chain, N_CONST)
                    for t in range(t0, t1):
                        if t >= 2:
                            pe.wait_ge(v_set, TH * own + t - 1)
                        nc.tensor.matmul(ybank[(t + 1) % 2][:ROWS[t], :], keysel[:, t * P:t * P + ROWS[t]],
                                         Vn[:, :, :].rearrange("m w d -> m (w d)"), start=True, stop=True
                                         ).then_inc(v_done, 1)

                def mlp_in(f):
                    if f == 0:
                        pe.wait_ge(x2T_lo_set, KT * n)
                    if f >= 2:
                        pe.wait_ge(gelu_done, FT * (n - 1) + f - 1)
                    elif b:
                        pe.wait_ge(exp_done, NT * n + NT - 1 + f)
                    cols = slice(f * P, (f + 1) * P)
                    for k in range(KT):
                        for part in (x2T_hi, x2T_lo):
                            ins = nc.tensor.matmul(ring[f % 2][:, :], W1T[:, k, cols], part[:, k, :],
                                                   start=(k == 0 and part is x2T_hi),
                                                   stop=(k == KT - 1 and part is x2T_lo))
                    ins.then_inc(f1_done, 1)

                def attend(s):
                    if s == 0:
                        pe.wait_ge(p_lo_set, NT * (n + 1))
                        if second:
                            pe.wait_ge(v_ones_set, 1 + TH)
                        pe.wait_ge(v_set, TH * (own + 1))
                    if s:
                        pe.wait_ge(o_set, SUB * n + s)
                    for h in range(KT):
                        for i in range(TH):
                            r, (h0, h1) = ROWS[i], HEADS_OF[i]
                            for part, w in ((p_hi, 0), (p_lo, 0), (p_hi, 1)):
                                ins = nc.tensor.matmul(
                                    o_ps[:, (h * HH + h0) * VH:(h * HH + h1) * VH],
                                    part[:r, h * TH + i, s * P:(s + 1) * P],
                                    V_s[:r, i, w, h, h0:h1, :].rearrange("p h c -> p (h c)"),
                                    start=(h == 0 and i == 0 and part is p_hi and w == 0),
                                    stop=(h == KT - 1 and i == TH - 1 and w == 1), skip_group_check=True)
                    ins.then_inc(pv_done, 1)

                def max_scores(g):
                    s, hh = divmod(g, 2 * KT)
                    h, i = divmod(hh, 2)
                    if g == 0:
                        pe.wait_ge(q_hi_set, KT * (n + 2))
                        if batch is not None:
                            pe.wait_ge(k_masked, KT * (batch + 1))
                            pe.wait_ge(k_hi_set, batch + 1)
                    if g >= 2:
                        pe.wait_ge(mx_red, NMX * (n + 1) + g - 1)
                    nc.tensor.matmul(mxb[g % 2][:, 0:HK // 2], qT_hi[:, h, s * P:(s + 1) * P],
                                     K_hi[:, h, i * (HK // 2):(i + 1) * (HK // 2)], start=True, stop=True
                                     ).then_inc(mx_done, 1)

                def project(s):
                    if s == 0:
                        pe.wait_ge(oT_lo_set, KT * (n + 1))
                        if second:
                            pe.wait_ge(wo_lo_set, 1)
                    if s < 2:
                        if c:
                            pe.wait_ge(y_set, SUB * (n - 1) + s + 1)
                    else:
                        pe.wait_ge(x2_set, SUB * n + s - 1)
                    cols = slice(s * P, (s + 1) * P)
                    for k in range(KT):
                        o = ybank[s % 2][:, 0:D]
                        nc.tensor.matmul(o, oT_hi[:, k, cols], Wo_hi[:, k, :], start=(k == 0), stop=False)
                        nc.tensor.matmul(o, oT_lo[:, k, cols], Wo_hi[:, k, :], start=False, stop=False)
                        ins = nc.tensor.matmul(o, oT_hi[:, k, cols], Wo_lo[:, k, :], start=False, stop=(k == KT - 1))
                    ins.then_inc(wo_done, 1)

                def mlp_out(s):
                    if s == 1:
                        if b:
                            pe.wait_ge(o_set, SUB * (n + 1))
                    elif s and b:
                        pe.wait_ge(x2_set, SUB * n + s + 1)
                    elif s:
                        pe.wait_ge(y_set, SUB * (n - 1) + s - 1)
                    cols = slice(s * P, (s + 1) * P)
                    for f in range(FT):
                        if s == 0 and f < EARLY:
                            pe.wait_ge(h_lo_set, EARLY * (n - 1) + f + 1)
                        elif s == 0:
                            pe.wait_ge(h_last_lo_set, 2 * (n - 1) + f - EARLY + 1)
                        for part in (h_hi, h_lo):
                            ins = nc.tensor.matmul(ybank[s % 2][:, 0:D], part[:, f, cols], W2T[:, f, :],
                                                   start=(f == 0 and part is h_hi), stop=(f == FT - 1 and part is h_lo))
                    ins.then_inc(f2_done, 1)

                def ternary_T():
                    for g in range(4 * KT):
                        if g < 2:
                            pe.wait_ge(exp_done, NT)
                        else:
                            pe.wait_ge(wt_set, g - 1)
                        pe.wait_ge(tern_set, 2 if g < 2 * KT else 4)
                        for j in range(4):
                            if g < 2 * KT:
                                src = W1_s[:, g % 2 * 4 + j, g // 2 * P:(g // 2 + 1) * P]
                            else:
                                q = g - 2 * KT
                                ft = q % 2 * 4 + j
                                src = W2_s[:, q // 2, ft * P:(ft + 1) * P]
                            ins = nc.tensor.transpose(ring[g % 2][:, j * P:(j + 1) * P], src, ident[:, :])
                        ins.then_inc(wt_done, 1)
                    pe.wait_ge(in_b1, 16)
                    pe.wait_ge(wt_set, 4 * KT - 1)
                    nc.tensor.transpose(ring[0][:, 0:FT], b1_r[:, :], ident[0:FT, 0:FT]).then_inc(wt_done, 1)

                def max_transposes():
                    pe.wait_ge(nm_set, n + 2)
                    if first:
                        pe.wait_ge(pool_chain, N_CONST)
                    for s in range(SUB):
                        ins = nc.tensor.transpose(mxb[0][0:2 * HEADS, s * P // 2:(s + 1) * P // 2].bitcast(BF16),
                                                  nmb[:, s, :], ident_b[:, :])
                    ins.then_inc(nmT_done, 1)

                if first:
                    pe.wait_ge(pool_chain, 2)
                    context_T()
                if b:
                    scores(0, 2)
                if c:
                    transposes(xn[1], xn_set[1], mxb, n - 1, x2T_done)
                if b:
                    scores(2, 4)
                if b and batch is not None:
                    context_T()
                if prep_v:
                    values()
                if b:
                    scores(4, 6)
                if a:
                    transposes(xn[0], xn_set[0], turn, n + 1, xT_done)
                if prep_v:
                    value_rows(0, 2)
                if b:
                    scores(6, 7)
                if batch is not None:
                    keys()
                if prep_v:
                    value_rows(2, 3)
                if b:
                    scores(7, 8)
                if prep_v:
                    value_rows(3, 4)
                if b:
                    scores(8, 9)
                if prep_v:
                    value_rows(4, TH)
                if b:
                    scores(9, NT)
                if a:
                    query()
                if second:
                    pe.wait_ge(v_set, TH)
                    pe.wait_ge(wabs_set, 2)
                    pe.wait_ge(ones_set, 1)
                    nc.tensor.matmul(y_ps[:, 0:2 * FT], ones[:, :], wabs[:, :, :].rearrange("p w f -> p (w f)"),
                                     start=True, stop=True).then_inc(wsum_done, 1)
                g = 0
                for r in range(SUB):
                    for i in range(3):
                        if c and i < 2:
                            mlp_in(2 * r + i)
                        if b and i == 2:
                            attend(r)
                        if a:
                            for _ in range(MAX_AFTER[r][i]):
                                max_scores(g)
                                g += 1
                if c:
                    mlp_out(0)
                if b:
                    if a:
                        pe.wait_ge(q_lo_set, KT * (n + 2))
                    transposes(o_s, o_set, turn, n, oT_done)
                if a:
                    max_transposes()
                if c:
                    mlp_out(1)
                if second:
                    pe.wait_ge(thr_step, 1)
                if b:
                    for s in range(SUB):
                        project(s)
                if c:
                    mlp_out(2)
                    mlp_out(3)
                if second:
                    ternary_T()
            steps(pe, step)


_INS = ["x", "ctx_1024", "mask_B_ik0", "g_xattn", "g_ffn", "L0_xattn_Wq", "L0_xattn_Wk", "L0_xattn_Wv", "L0_xattn_Wo",
        "L0_ffn_W1", "L0_ffn_b1", "L0_ffn_W2", "L0_ffn_b2"]


def kernel(**inputs):
    import numpy as _np
    import concourse.bacc as _bacc
    from concourse import mybir as _mybir
    from concourse.bass_utils import run_bass_kernel_spmd as _run

    nc = _bacc.Bacc("TRN2", target_bir_lowering=False, num_devices=1)
    arrays, args = {}, []
    for name in _INS:
        if name == "mask_B_ik0":
            continue
        a = _np.ascontiguousarray(inputs[name])
        arrays[f"in_{name}_dram"] = a
        args.append(nc.dram_tensor(f"in_{name}_dram", a.shape, _mybir.dt.from_np(a.dtype), kind="ExternalInput").ap())
    shape = inputs["x"].shape
    args.append(nc.dram_tensor("out_dram", shape, _mybir.dt.float32, kind="ExternalOutput").ap())
    gated_cross_attention_block(nc, *args)
    r = _run(nc, [arrays], core_ids=[0])
    return r.results[0]["out_dram"]
```

```python
from contextlib import ExitStack

import concourse.bass as bass
from concourse import mybir

F32 = mybir.dt.float32
F32R = mybir.dt.float32r
BF16 = mybir.dt.bfloat16
F16 = mybir.dt.float16
ALU = mybir.AluOpType
ACT = mybir.ActivationFunctionType
AX_X = mybir.AxisListType.X

P = 128
HEADS = 16
EPS = 1e-5


def gated_cross_attention_block(nc, x, ctx, g_xattn, g_ffn, Wq, Wk, Wv, Wo, W1, b1, W2, b2, out):
    B, S, D = x.shape
    NK = ctx.shape[1]
    FF = W1.shape[0]
    DH = D // HEADS
    KT = D // P
    HH = P // DH
    FT = FF // P
    BLK = 512
    NB = B * S // BLK
    BPB = S // BLK
    SUB = BLK // P
    HK = HH * NK
    TH = -(-HK // P)
    NT = KT * TH
    ROWS = [min(P, HK - t * P) for t in range(TH)]
    VH = DH + 1
    HEADS_OF = [(t * P // NK, (t * P + ROWS[t] - 1) // NK + 1) for t in range(TH)]
    NMX = SUB * KT * 2
    ORDER = "FFPMM FMMFMMP FMMFMMFMMP FMMMMP".replace(" ", "")
    FIRST_ORDER = "MMMMMMMMMM PMM PMM PMM P".replace(" ", "")
    EARLY_MAX = {5: 2, 6: 3, 7: 2, 8: 1, 9: 2}
    LAST_ORDER = "FFPFPFPFFPFFTYWWWWYYY"
    NW = FF * KT // 512
    P_LAST = NT - 2
    EARLY, EARLY_AT_END = FT - 1, FT - 2
    assert [ORDER.count(kind) for kind in "FMP"] == [FT, NMX, SUB]
    assert BPB == 2 and NB >= 6 and HK % 2 == 0 and NT % 2 == 0 and FT % 2 == 0

    x_v = x.rearrange("b t d -> (b t) d").rearrange("(n p s) d -> n p (s d)", p=P, s=SUB)
    out_v = out.rearrange("b t d -> (b t) d").rearrange("(n p s) d -> n p (s d)", p=P, s=SUB)

    with ExitStack() as stack:
        def sb(name, shape, dt=F32):
            return stack.enter_context(nc.sbuf_tensor(name, shape, dt))

        def psum(name):
            return stack.enter_context(nc.psum_tensor(name, [P, 512], F32))

        def sem(name):
            return stack.enter_context(nc.semaphore(name))

        ring = [psum("ring0"), psum("ring1")]
        turn = [psum("turn0"), psum("turn1")]
        mxb = [psum("mxb0"), psum("mxb1")]
        y_ps = psum("y_ps")
        ybank = [y_ps, psum("o_ps")]
        wt_banks = ring + ybank
        mx_banks = mxb + turn
        wo_banks = [turn[0], turn[1], mxb[1], mxb[0]]

        ident = sb("ident", [P, P])
        ident_b = sb("ident_b", [P, P], BF16)
        ones = sb("ones", [P, P])
        kmask = sb("kmask", [P, HH])
        vmask = sb("vmask", [P, TH, HH])
        headsel = sb("headsel", [2 * HEADS, KT, HK], BF16)
        keysel = sb("keysel", [NK, HK], F16)
        neg_half = sb("neg_half", [P, SUB])
        Wk_s = sb("Wk_s", [P, KT, D])
        Wv_s = sb("Wv_s", [P, KT, D])
        Wq_s = sb("Wq_s", [P, KT, D])
        Wo_s = sb("Wo_s", [P, KT, D])
        Wq_hi, Wq_lo = sb("Wq_hi", [P, KT, D], F32R), sb("Wq_lo", [P, KT, D], F32R)
        Wo_hi, Wo_lo = sb("Wo_hi", [P, KT, D], F32R), sb("Wo_lo", [P, KT, D], F32R)
        W1T = sb("W1T", [P, KT, FF], F32R)
        W2T = sb("W2T", [P, FT, D], F32R)
        b1_r = sb("b1_r", [FT, P])
        b1_s = sb("b1_s", [P, FT])
        b2_s = sb("b2_s", [P, D])
        b2_g = sb("b2_g", [P, D])
        gates = sb("gates", [P, 2])
        tg = sb("tg", [P, 2])
        wabs = sb("wabs", [P, 2, NW])
        wsum = sb("wsum", [P, 2])
        wscale = sb("wscale", [P, 2])
        thr = sb("thr", [P, 2, 2])

        ctx_s = sb("ctx_s", [NK, D])
        ctxT = sb("ctxT", [P, KT, NK])
        K_f = sb("K_f", [P, KT, HK])
        K_hi, K_lo = sb("K_hi", [P, KT, HK], F32R), sb("K_lo", [P, KT, HK], F32R)
        Vn = sb("Vn", [NK, 2, D], F16)
        V_s = sb("V_s", [P, TH, 2, KT, HH, VH], F16)

        xb = [sb(f"xb{i}", [P, SUB, D]) for i in range(2)]
        xr = sb("xr", [P, SUB, D])
        stats = [sb(f"stats{i}", [P, SUB, 6]) for i in range(2)]
        lnp = [sb(f"lnp{i}", [P, 6, SUB]) for i in range(2)]
        table = sb("table", [1, 4])
        rstd = [sb(f"rstd{i}", [P, SUB]) for i in range(2)]
        shift = [sb(f"shift{i}", [P, SUB]) for i in range(2)]
        xn = [sb(f"xn{i}", [P, SUB, D]) for i in range(2)]
        xT_hi, xT_lo = sb("xT_hi", [P, KT, BLK], F32R), sb("xT_lo", [P, KT, BLK], F32R)
        qT_hi, qT_lo = sb("qT_hi", [P, KT, BLK], F32R), sb("qT_lo", [P, KT, BLK], F32R)
        nm = sb("nm", [P, SUB, HEADS])
        nmb = sb("nmb", [P, SUB, 2 * HEADS], BF16)
        nmT = sb("nmT", [2 * HEADS, BLK], BF16)
        PR = NT // 2
        probs = sb("probs", [P, PR, BLK])
        p_hi, p_lo = sb("p_hi", [P, NT, BLK], F16), sb("p_lo", [P, NT, BLK], F16)
        rz = [sb(f"rz{i}", [P, HEADS]) for i in range(2)]
        o_s = sb("o_s", [P, SUB, D])
        oT_hi, oT_lo = xT_hi, xT_lo
        x2 = sb("x2", [P, SUB, D])
        x2T_hi, x2T_lo = sb("x2T_hi", [P, KT, BLK], F32R), sb("x2T_lo", [P, KT, BLK], F32R)
        first_qT = x2T_hi, x2T_lo
        h_f = sb("h_f", [P, FT, BLK])
        w12 = h_f[:, :, :].rearrange("p f n -> p (f n)")
        W1_s = w12[:, 0:FT * D].rearrange("p (f n) -> p f n", n=D)
        W2_s = w12[:, FT * D:].rearrange("p (k n) -> p k n", n=FF)
        h_hi, h_lo = sb("h_hi", [P, FT, BLK], F32R), sb("h_lo", [P, FT, BLK], F32R)
        y = [sb(f"y{i}", [P, SUB, D]) for i in range(2)]
        tneg = y[1][:, :, :].rearrange("p s d -> p (s d)")

        in_x = [sem(f"in_x{i}") for i in range(2)]
        in_first = sem("in_first")
        in_r = sem("in_r")
        in_ctx = sem("in_ctx")
        in_wq, in_wk, in_wv, in_wo = sem("in_wq"), sem("in_wk"), sem("in_wv"), sem("in_wo")
        in_w1, in_w2, in_b1, in_b2, in_g = sem("in_w1"), sem("in_w2"), sem("in_b1"), sem("in_b2"), sem("in_g")
        pool_chain = sem("pool_chain")
        ones_set = sem("ones_set")
        tg_set, b2_set = sem("tg_set"), sem("b2_set")
        table_set = sem("table_set")
        wq_hi_set, wq_lo_set, wo_hi_set, wo_lo_set = (sem(f"{w}_set") for w in ("wq_hi", "wq_lo", "wo_hi", "wo_lo"))
        wabs_set, wsum_done, thr_step = sem("wabs_set"), sem("wsum_done"), sem("thr_step")
        tneg_set, tern_set = sem("tneg_set"), sem("tern_set")
        wt_done, wt_set = sem("wt_done"), sem("wt_set")
        b1_done, b1_set = sem("b1_done"), sem("b1_set")
        ctxT_done, ctxT_set, kT_done, k_masked, k_hi_set, k_lo_set = (
            sem(s) for s in ("ctxT_done", "ctxT_set", "kT_done", "k_masked", "k_hi_set", "k_lo_set"))
        vn_done, vn_hi_set, vn_set = sem("vn_done"), sem("vn_hi_set"), sem("vn_set")
        v_done, v_set, v_ones_set = sem("v_done"), sem("v_set"), sem("v_ones_set")
        st_set, half_set, mean_set, sq_set, var_set, ve_set, rstd_set, shift_set, xn_set = (
            [sem(f"{s}{i}") for i in range(2)]
            for s in ("st_set", "half_set", "mean_set", "sq_set", "var_set", "ve_set", "rstd_set", "shift_set", "xn_set"))
        xT_done, xT_hi_set, xT_lo_set = sem("xT_done"), sem("xT_hi_set"), sem("xT_lo_set")
        q_done, q_hi_set, q_lo_set = sem("q_done"), sem("q_hi_set"), sem("q_lo_set")
        mx_done, mx_red, nm_hi_set, nm_set = sem("mx_done"), sem("mx_red"), sem("nm_hi_set"), sem("nm_set")
        nmT_done, nmT_set = sem("nmT_done"), sem("nmT_set")
        s_done, exp_done, p_hi_set, p_lo_set, p_last_lo_set, pv_done, rz_set, o_set = (
            sem(s) for s in ("s_done", "exp_done", "p_hi_set", "p_lo_set", "p_last_lo_set", "pv_done", "rz_set", "o_set"))
        oT_done, oT_hi_set, oT_lo_set = sem("oT_done"), sem("oT_hi_set"), sem("oT_lo_set")
        wo_done, x2_set, y_base = sem("wo_done"), sem("x2_set"), sem("y_base")
        x2T_done, x2T_hi_set, x2T_lo_set = sem("x2T_done"), sem("x2T_hi_set"), sem("x2T_lo_set")
        f1_done, gelu_done, h_hi_set, h_lo_set, h_last_hi_set, h_last_lo_set, f2_done, y_set = (
            sem(s) for s in ("f1_done", "gelu_done", "h_hi_set", "h_lo_set", "h_last_hi_set", "h_last_lo_set",
                             "f2_done", "y_set"))
        last_stored = sem("last_stored")
        y_free = [sem(f"y_free{i}") for i in range(2)]

        def low_tiles(n, a, b):
            done = (EARLY * (n - 1), (FT - EARLY) * (n - 1)) if b else (
                EARLY * (n - 2) + EARLY_AT_END, (FT - EARLY) * (n - 2) + FT - EARLY_AT_END)
            return EARLY if a else EARLY_AT_END, *done

        N_CONST = 15

        def steps(eng, step):
            step(-1, 1, True, True, False, False, -1, 0)
            step(0, 0, True, True, True, False, 0, None)
            with eng.Fori(0, NB // 2 - 2) as i:
                step(2 * i + 1, 1, True, True, True, True, i, i + 1)
                step(2 * i + 2, 0, True, True, True, True, i + 1, None)
            step(NB - 3, 1, True, True, True, True, NB // 2 - 2, NB // 2 - 1)
            step(NB - 2, 0, False, True, True, True, NB // 2 - 1, None)
            step(NB - 1, 1, False, False, True, True, NB // 2 - 1, None)
            step(NB, 0, False, False, False, True, NB // 2, None)

        block = stack.enter_context(nc.Block())

        @block.sync
        def _(sp):
            for half, w_in in ((slice(0, SUB // 2), in_first), (slice(SUB // 2, SUB), in_x[0])):
                sp.dma_start(xb[0][:, half, :], x_v[0].rearrange("p (s d) -> p s d", s=SUB)[:, half, :]).then_inc(w_in, 16)
            sp.dma_start(ctx_s[:, :], ctx[0]).then_inc(in_ctx, 16)
            def weight(w, w_s, w_in):
                sp.dma_start(w_s[:, :, :], w.rearrange("(k p) n -> p k n", p=P)).then_inc(w_in, 16)
            weight(Wq, Wq_s, in_wq)
            weight(Wk, Wk_s, in_wk)
            weight(W1, W1_s, in_w1)
            sp.dma_start(b1_r[:, :], b1.rearrange("(f p) -> f p", p=P)).then_inc(in_b1, 16)
            sp.dma_start(gates[:, 0:1], g_xattn.partition_broadcast(P)).then_inc(in_g, 16)
            sp.dma_start(gates[:, 1:2], g_ffn.partition_broadcast(P)).then_inc(in_g, 16)
            sp.dma_start(xb[1][:, :, :], x_v[1].rearrange("p (s d) -> p s d", s=SUB)).then_inc(in_x[1], 16)
            weight(W2, W2_s, in_w2)
            weight(Wo, Wo_s, in_wo)
            weight(Wv, Wv_s, in_wv)
            sp.dma_start(b2_s[:, :], b2.partition_broadcast(P)).then_inc(in_b2, 16)

            def step(n, par, ahead, a, b, c, own, batch):
                if b and ahead:
                    sp.wait_ge(xn_set[0], SUB * (n + 1))
                    sp.dma_start(xb[par][:, :, :], x_v[n + 2].rearrange("p (s d) -> p s d", s=SUB)
                                 ).then_inc(in_x[par], 16)
                if b and batch is not None:
                    sp.wait_ge(ctxT_done, batch)
                    sp.dma_start(ctx_s[:, :], ctx[batch]).then_inc(in_ctx, 16)
                if b and c:
                    sp.wait_ge(x2_set, SUB * n)
                if b:
                    sp.dma_start(xr[:, :, :], x_v[n].rearrange("p (s d) -> p s d", s=SUB)).then_inc(in_r, 16)
                if c and not b:
                    for part, stored in ((slice(0, SUB - 1), y_free[1 - par]), (slice(SUB - 1, SUB), last_stored)):
                        sp.wait_ge(y_set, SUB * (n - 1) + part.stop)
                        sp.dma_start(out_v[n - 1].rearrange("p (s d) -> p s d", s=SUB)[:, part, :], y[1 - par][:, part, :]
                                     ).then_inc(stored, 16)
                elif c:
                    sp.wait_ge(y_set, SUB * n)
                    sp.dma_start(out_v[n - 1].rearrange("p (s d) -> p s d", s=SUB), y[1 - par][:, :, :]
                                 ).then_inc(y_free[1 - par], 16)
            steps(sp, step)
            for par in range(2):
                sp.wait_ge(y_free[par], 16 * (NB // 2 + 1))
            sp.wait_ge(last_stored, 16)

        @block.gpsimd
        def _(pool):
            done = [0]

            def chain(ins):
                done[0] += 1
                ins.then_inc(pool_chain, 1)
                return done[0]

            def band(t, pattern, width):
                pool.wait_ge(pool_chain, chain(nc.gpsimd.affine_select(
                    out=t, in_=t, pattern=[[-s, c] for s, c in pattern], compare_op=ALU.is_ge, fill=0.0,
                    base=0, channel_multiplier=1)))
                return chain(nc.gpsimd.affine_select(
                    out=t, in_=t, pattern=pattern, compare_op=ALU.is_ge, fill=0.0,
                    base=width - 1, channel_multiplier=-1))

            def diagonal(t, pattern, base):
                return chain(nc.gpsimd.affine_select(
                    out=t, in_=t, pattern=pattern, compare_op=ALU.not_equal, fill=1.0,
                    base=base, channel_multiplier=-1))

            pool.wait_ge(pool_chain, chain(nc.gpsimd.memset(ident[:, :], 0.0)))
            diagonal(ident[:, :], [[1, P]], 0)
            chain(nc.gpsimd.memset(neg_half[:, :], -0.5))
            for i in range(2):
                nc.gpsimd.memset(y[i][:, 0, 0:1], 0.0).then_inc(y_free[i], 16)
            pool.wait_ge(pool_chain, chain(nc.gpsimd.memset(kmask[:, :], 1.0)))
            band(kmask[:, :], [[DH, HH]], DH)

            def inverse_deviation(which, blk):
                pool.wait_ge(ve_set[which], blk + 1)
                nc.gpsimd.tensor_tensor(rstd[which][:, :], lnp[which][:, 5, :], neg_half[:, :], ALU.pow
                                        ).then_inc(rstd_set[which], 1)
                pool.wait_ge(mean_set[which], blk + 1)
                pool.wait_ge(rstd_set[which], blk + 1)
                nc.gpsimd.tensor_tensor(shift[which][:, :], lnp[which][:, 3, :], rstd[which][:, :], ALU.mult
                                        ).then_inc(shift_set[which], 1)

            def prepare():
                pool.wait_ge(in_wq, 16)
                pool.wait_ge(wq_hi_set, 1)
                nc.gpsimd.tensor_tensor(Wq_lo[:, :, :], Wq_s[:, :, :], Wq_hi[:, :, :].bitcast(F32), ALU.subtract
                                        ).then_inc(wq_lo_set, 1)
                pool.wait_ge(pool_chain, chain(nc.gpsimd.memset(vmask[:, :, :], 1.0)))
                pool.wait_ge(pool_chain, chain(nc.gpsimd.affine_select(
                    out=vmask[:, :, :], in_=vmask[:, :, :], pattern=[[P, TH], [-NK, HH]], compare_op=ALU.is_ge,
                    fill=0.0, base=0, channel_multiplier=1)))
                chain(nc.gpsimd.affine_select(
                    out=vmask[:, :, :], in_=vmask[:, :, :], pattern=[[-P, TH], [NK, HH]], compare_op=ALU.is_ge,
                    fill=0.0, base=NK - 1, channel_multiplier=-1))
                sel = headsel[:, :, :].rearrange("r k (h m) -> r k h m", h=HH)
                pool.wait_ge(pool_chain, chain(nc.gpsimd.memset(sel, 0.0)))
                pool.wait_ge(pool_chain, diagonal(sel, [[HH, KT], [1, HH], [0, NK]], 0))
                diagonal(sel, [[HH, KT], [1, HH], [0, NK]], HEADS)
                chain(nc.gpsimd.tensor_copy(ident_b[:, :], ident[:, :]))
                by_key = keysel[:, :].rearrange("r (h m) -> r h m", h=HH)
                pool.wait_ge(pool_chain, chain(nc.gpsimd.memset(by_key, 0.0)))
                diagonal(by_key, [[0, HH], [1, NK]], 0)
                assert done[0] == N_CONST, done
                inverse_deviation(0, 1)
                pool.wait_ge(wo_hi_set, 1)
                nc.gpsimd.tensor_tensor(Wo_lo[:, :, :], Wo_s[:, :, :], Wo_hi[:, :, :].bitcast(F32), ALU.subtract
                                        ).then_inc(wo_lo_set, 1)
                pool.wait_ge(in_b2, 16)
                pool.wait_ge(tg_set, 1)
                nc.gpsimd.tensor_scalar(b2_g[:, :], b2_s[:, :], tg[:, 1:2], None, ALU.mult).then_inc(b2_set, 1)

            def step(n, par, ahead, a, b, c, own, batch):
                first, second, last = not b and not c, b and not c, b and not a
                prep_v = b and par == 0
                if first:
                    pool.wait_ge(pool_chain, 3)
                    inverse_deviation(0, n + 1)
                if first:
                    prepare()
                if b:
                    tiles = NT if a and c else P_LAST
                    for t in range(tiles):
                        pool.wait_ge(p_hi_set, NT * n + t + 1)
                        rows = ROWS[t % TH]
                        nc.gpsimd.tensor_tensor(p_lo[:rows, t, :], probs[:rows, t % PR, :], p_hi[:rows, t, :], ALU.subtract
                                                ).then_inc(p_lo_set, 1 if t < tiles - 1 else 1 + NT - tiles)
                    if ahead:
                        inverse_deviation(0, n + 2)
                if c:
                    pool.wait_ge(y_free[1 - par], 16 * (own + par))
                    nc.gpsimd.tensor_tensor(y[1 - par][:, :, :], x2[:, :, :],
                                            b2_g[:, :].unsqueeze(1).broadcast_to([P, SUB, D]), ALU.add
                                            ).then_inc(y_base, 1)
                    for f in range(low_tiles(n, a, b)[0]):
                        pool.wait_ge(h_hi_set, (FT - 1) * (n - 1) + f + 1)
                        nc.gpsimd.tensor_tensor(h_lo[:, f, :], h_f[:, f, :], h_hi[:, f, :].bitcast(F32), ALU.subtract
                                                ).then_inc(h_lo_set, 1)
                if batch is not None:
                    pool.wait_ge(k_hi_set, batch + 1)
                    nc.gpsimd.tensor_tensor(K_lo[:, :, :], K_f[:, :, :], K_hi[:, :, :].bitcast(F32), ALU.subtract
                                            ).then_inc(k_lo_set, 1)
                if b:
                    inverse_deviation(1, n)
                    if second:
                        pool.wait_ge(b2_set, 1)
            steps(pool, step)

        @block.scalar
        def _(act):
            def copy(dst, src, done):
                nc.scalar.activation(dst, src, ACT.Copy).then_inc(done, 1)

            def normalize(which, blk, src, s0, s1, transposed):
                if s0 == 0:
                    act.wait_ge(shift_set[which], blk + 1)
                    if transposed:
                        act.wait_ge(transposed, KT * blk)
                for s in range(s0, s1):
                    nc.scalar.activation(xn[which][:, s, :], src[:, s, :], ACT.Identity, bias=shift[which][:, s:s + 1],
                                         scale=rstd[which][:, s:s + 1]).then_inc(xn_set[which], 1)

            def weight_sizes(w, w_s, loaded):
                act.wait_ge(loaded, 16)
                flat = w_s[:, :, :].rearrange("p k n -> p (k n)")
                for i in range(NW):
                    if w:
                        act.wait_ge(wabs_set, NW + i)
                    nc.scalar.activation(probs[:, i % PR, :], flat[:, i * 512:(i + 1) * 512], ACT.Abs,
                                         accum_out=wabs[:, w, i:i + 1]).then_inc(wabs_set, 1)

            def fetch_table(func, fetched):
                act.wait_ge(table_set, fetched + 1)
                nc.scalar.activation(table[:, 1:2], table[:, 0:1], func).then_inc(table_set, 1)

            act.wait_ge(in_wq, 16)
            copy(Wq_hi[:, :, :], Wq_s[:, :, :], wq_hi_set)
            act.wait_ge(in_g, 32)
            nc.scalar.activation(tg[:, :], gates[:, :], ACT.Tanh).then_inc(tg_set, 1)

            def step(n, par, ahead, a, b, c, own, batch):
                first, second, last = not b and not c, b and not c, b and not a
                prep_v = b and par == 0
                def scores(t0, t1):
                    for t in range(t0, t1):
                        rows = ROWS[t % TH]
                        act.wait_ge(s_done, NT * n + t + 1)
                        if c or t >= PR:
                            act.wait_ge(p_lo_set, NT * n + t - PR + 1)
                        nc.scalar.activation(probs[:rows, t % PR, :], ring[t % 2][:rows, :], ACT.Exp
                                             ).then_inc(exp_done, 1)
                        if second:
                            act.wait_ge(exp_done, t + 1)
                            copy(p_hi[:rows, t, :], probs[:rows, t % PR, :], p_hi_set)

                def high_part(dst, bank, blk, done, hi_set, h):
                    act.wait_ge(done, KT * blk + h + 1)
                    copy(dst[:, h, :], bank[h][:, :], hi_set)

                def gelu(f):
                    act.wait_ge(f1_done, FT * (n - 1) + f + 1)
                    nc.scalar.activation(h_f[:, f, :], ring[f % 2][:, :], ACT.Gelu, bias=b1_s[:, f:f + 1]
                                         ).then_inc(gelu_done, 1)

                def weights_T(w):
                    for g in range(2 * KT * w, 2 * KT * (w + 1)):
                        act.wait_ge(wt_done, g + 1)
                        src = wt_banks[g % 4][:, :]
                        if w == 0:
                            dst = W1T[:, g // 2, g % 2 * 512:g % 2 * 512 + 512]
                        else:
                            dst = W2T[:, :, :].rearrange("p (q f) (k d) -> p k q f d", q=2, k=KT)[:, g // 2 - KT, g % 2]
                            src = src.rearrange("p (f d) -> p f d", d=P)
                        copy(dst, src, wt_set)

                def h_high(f):
                    act.wait_ge(gelu_done, FT * (n - 1) + f + 1)
                    copy(h_hi[:, f, :], h_f[:, f, :], h_hi_set)

                if b:
                    scores(0, 1)
                if c:
                    normalize(1, n - 1, x2, 0, 1, x2T_done)
                if b:
                    scores(1, 2)
                if c:
                    normalize(1, n - 1, x2, 1, SUB if b else SUB // 2, None)
                if a:
                    if c:
                        act.wait_ge(wo_done, SUB * n)
                    high_part(xT_hi, turn, n + 1, xT_done, xT_hi_set, 0)
                if second:
                    high_part(xT_hi, turn, n + 1, xT_done, xT_hi_set, 1)
                if b:
                    scores(2, 3)
                if a and not second:
                    high_part(xT_hi, turn, n + 1, xT_done, xT_hi_set, 1)
                if first:
                    weight_sizes(0, W1_s, in_w1)
                    act.wait_ge(k_masked, KT)
                    copy(K_hi[:, :, :], K_f[:, :, :], k_hi_set)
                if b:
                    scores(3, 5)
                if second:
                    for h in range(KT):
                        high_part(qT_hi, turn, n + 1, q_done, q_hi_set, h)
                if c:
                    high_part(x2T_hi, mxb, n - 1, x2T_done, x2T_hi_set, 0)
                if b:
                    scores(5, 6)
                if c:
                    high_part(x2T_hi, mxb, n - 1, x2T_done, x2T_hi_set, 1)
                if b:
                    scores(6, NT)
                if c and b:
                    fetch_table(ACT.Gelu, 2 * n - 2)
                if a and not second:
                    for h in range(KT):
                        if b and h == 0:
                            act.wait_ge(mx_done, NMX * (n + 1))
                        high_part(first_qT[0] if first else qT_hi, turn, n + 1, q_done, q_hi_set, h)
                if first:
                    act.wait_ge(b1_done, 1)
                    copy(b1_s[:, :], ring[0][:, 0:FT], b1_set)
                    act.wait_ge(in_wo, 16)
                    copy(Wo_hi[:, :, :], Wo_s[:, :, :], wo_hi_set)
                    weight_sizes(1, W2_s, in_w2)
                if c:
                    for f in range(FT):
                        gelu(f)
                        if f and b:
                            h_high(f - 1)
                    if b and a:
                        fetch_table(ACT.Exp, 2 * n - 1)
                if b:
                    if a:
                        act.wait_ge(q_done, KT * (n + 2))
                    for h in range(KT):
                        high_part(oT_hi, turn, n, oT_done, oT_hi_set, h)
                    if second:
                        weights_T(0)
                if ahead:
                    normalize(0, n + 2, xb[par], 0, SUB, xT_done)
                if second:
                    weights_T(1)
            steps(act, step)

        @block.vector
        def _(dve):
            def subtile_statistics(which, s, src):
                nc.vector.bn_stats(stats[which][:, s, :], src[:, s, :]).then_inc(st_set[which], 1)

            def statistics(which, blk):
                diff, total, m2, minus_mean, sq, ve = (lnp[which][:, i, :] for i in range(6))
                dve.wait_ge(st_set[which], SUB * (blk + 1))
                even, odd = stats[which][:, :, 0:3], stats[which][:, :, 3:6]
                nc.vector.tensor_tensor(diff, even[:, :, 1], odd[:, :, 1], ALU.subtract).then_inc(half_set[which], 1)
                nc.vector.tensor_tensor(total, even[:, :, 1], odd[:, :, 1], ALU.add).then_inc(half_set[which], 1)
                nc.vector.tensor_tensor(m2, even[:, :, 2], odd[:, :, 2], ALU.add).then_inc(half_set[which], 1)
                dve.wait_ge(half_set[which], 3 * (blk + 1))
                nc.vector.scalar_tensor_tensor(sq, diff, D / 4, diff, ALU.mult, ALU.mult).then_inc(sq_set[which], 1)
                nc.vector.tensor_scalar(minus_mean, total, -0.5, None, ALU.mult).then_inc(mean_set[which], 1)
                dve.wait_ge(sq_set[which], blk + 1)
                nc.vector.tensor_tensor(diff, sq, m2, ALU.add).then_inc(var_set[which], 1)
                dve.wait_ge(var_set[which], blk + 1)
                nc.vector.tensor_scalar(ve, diff, 1.0 / D, EPS, ALU.mult, ALU.add).then_inc(ve_set[which], 1)

            def normalize(which, src, s0, s1):
                for s in range(s0, s1):
                    nc.vector.tensor_scalar(xn[which][:, s, :], src[:, s, :], rstd[which][:, s:s + 1],
                                            shift[which][:, s:s + 1], ALU.mult, ALU.add).then_inc(xn_set[which], 1)

            def low_part(dst, hi, bank, blk, hi_set, lo_set, h):
                dve.wait_ge(hi_set, KT * blk + h + 1)
                nc.vector.tensor_tensor(dst[:, h, :], bank[h][:, :], hi[:, h, :].bitcast(F32), ALU.subtract
                                        ).then_inc(lo_set, 1)

            nc.vector.memset(table[:, :], 0.0).then_inc(table_set, 1)
            nc.vector.memset(ones[:, :], 1.0).then_inc(ones_set, 1)
            for t, (h0, h1) in enumerate(HEADS_OF):
                nc.vector.memset(V_s[:, t].rearrange("p w k h c -> p (w k) h c")[:, :, h0:h1, :], 0.0
                                 ).then_inc(v_ones_set, 1)

            def step(n, par, ahead, a, b, c, own, batch):
                first, second, last = not b and not c, b and not c, b and not a
                prep_v = b and par == 0
                def context_T():
                    dve.wait_ge(ctxT_done, batch + 1)
                    if b:
                        dve.wait_ge(vn_done, batch)
                    nc.vector.tensor_copy(ctxT[:, :, :], mxb[0][:, 0:KT * P].rearrange("p (k c) -> p k c", k=KT)[:, :, 0:NK]
                                          ).then_inc(ctxT_set, 1)

                def keys():
                    dve.wait_ge(kT_done, batch + 1)
                    if first:
                        dve.wait_ge(pool_chain, 6)
                    for k in range(KT):
                        src = mxb[1][:, k * P:k * P + NK].unsqueeze(1).broadcast_to([P, HH, NK])
                        msk = kmask[:, :].unsqueeze(2).broadcast_to([P, HH, NK])
                        nc.vector.tensor_tensor(K_f[:, k, :].rearrange("p (h m) -> p h m", h=HH), src, msk, ALU.mult
                                                ).then_inc(k_masked, 1)

                def keys_high():
                    dve.wait_ge(s_done, NT * (n + 1))
                    dve.wait_ge(k_masked, KT * (batch + 1))
                    nc.vector.tensor_copy(K_hi[:, :, :], K_f[:, :, :]).then_inc(k_hi_set, 1)

                def values():
                    dve.wait_ge(vn_done, own + 1)
                    if c:
                        dve.wait_ge(v_done, TH * own)
                    nc.vector.tensor_copy(Vn[:, 0, :], y_ps[0:NK, 0:D]).then_inc(vn_hi_set, 1)
                    dve.wait_ge(vn_hi_set, own + 1)
                    nc.vector.tensor_tensor(Vn[:, 1, :], y_ps[0:NK, 0:D], Vn[:, 0, :], ALU.subtract
                                            ).then_inc(vn_set, 1)

                def value_rows(t0, t1):
                    for t in range(t0, t1):
                        dve.wait_ge(v_done, TH * own + t + 1)
                        if c and t == 0:
                            dve.wait_ge(pv_done, SUB * n)
                        if second and t == 0:
                            dve.wait_ge(pool_chain, N_CONST)
                            dve.wait_ge(v_ones_set, TH)
                        r = ROWS[t]
                        h0, h1 = HEADS_OF[t]
                        nh = h1 - h0
                        dst = V_s[:r, t].rearrange("p w k h c -> p (w k) h c")[:, :, h0:h1, 0:DH]
                        src = ybank[(t + 1) % 2][:r, 0:2 * KT * nh * DH].rearrange("p (w h d) -> p w h d", w=2 * KT, h=nh)
                        msk = vmask[:r, t, h0:h1].unsqueeze(1).unsqueeze(3).broadcast_to([r, 2 * KT, nh, DH])
                        nc.vector.tensor_tensor(dst, src, msk, ALU.mult).then_inc(v_set, 1)
                        if second:
                            nc.vector.tensor_copy(V_s[:, t, 0, :, h0:h1, DH],
                                                  vmask[:, t, h0:h1].unsqueeze(1).broadcast_to([P, KT, nh])).then_inc(v_ones_set, 1)

                def p_high(t):
                    rows = ROWS[t % TH]
                    dve.wait_ge(exp_done, NT * n + t + 1)
                    if t == 0 and c:
                        dve.wait_ge(pv_done, SUB * n)
                    nc.vector.tensor_copy(p_hi[:rows, t, :], probs[:rows, t % PR, :]).then_inc(p_hi_set, 1)

                def p_low():
                    if second or last:
                        for t in range(P_LAST, NT):
                            rows = ROWS[t % TH]
                            dve.wait_ge(p_hi_set, NT * n + t + 1)
                            nc.vector.tensor_tensor(p_lo[:rows, t, :], probs[:rows, t % PR, :], p_hi[:rows, t, :],
                                                    ALU.subtract).then_inc(p_last_lo_set, 1)

                def h_low(f):
                    if f == FT - 1:
                        dve.wait_ge(gelu_done, FT * n)
                        nc.vector.tensor_copy(h_hi[:, f, :], h_f[:, f, :]).then_inc(h_last_hi_set, 1)
                        dve.wait_ge(h_last_hi_set, n)
                    else:
                        dve.wait_ge(h_hi_set, (FT - 1) * (n - 1) + f + 1)
                    nc.vector.tensor_tensor(h_lo[:, f, :], h_f[:, f, :], h_hi[:, f, :].bitcast(F32), ALU.subtract
                                            ).then_inc(h_last_lo_set, 1)

                def head_outputs(s):
                    dve.wait_ge(pv_done, SUB * n + s + 1)
                    o_v = ybank[s % 2][:, 0:HEADS * VH].rearrange("p (h c) -> p h c", c=VH)
                    nc.vector.reciprocal(rz[s % 2][:, :], o_v[:, :, DH]).then_inc(rz_set, 1)
                    dve.wait_ge(rz_set, SUB * n + s + 1)
                    nc.vector.tensor_tensor(
                        o_s[:, s, :].rearrange("p (h d) -> p h d", h=HEADS), o_v[:, :, 0:DH],
                        rz[s % 2][:, :].unsqueeze(2).broadcast_to([P, HEADS, DH]), ALU.mult).then_inc(o_set, 1)

                def maxima(g):
                    s, hh = divmod(g, 2 * KT)
                    dve.wait_ge(mx_done, NMX * (n + 1) + g + 1)
                    nc.vector.tensor_reduce(nm[:, s, hh * (HH // 2):(hh + 1) * (HH // 2)],
                                            mx_banks[g % 4][:, 0:HK // 2].rearrange("p (h m) -> p h m", m=NK),
                                            AX_X, ALU.max,
                                            negate=True).then_inc(mx_red, 1)

                def max_parts():
                    dve.wait_ge(mx_red, NMX * (n + 2))
                    nc.vector.tensor_copy(nmb[:, :, 0:HEADS], nm[:, :, :]).then_inc(nm_hi_set, 1)
                    dve.wait_ge(nm_hi_set, n + 2)
                    nc.vector.tensor_tensor(nmb[:, :, HEADS:], nm[:, :, :], nmb[:, :, 0:HEADS], ALU.subtract
                                            ).then_inc(nm_set, 1)

                def residual(s):
                    dve.wait_ge(wo_done, SUB * n + s + 1)
                    if s == 0:
                        dve.wait_ge(in_r, 16 * (n + 1))
                    if c and s == 0:
                        dve.wait_ge(xn_set[1], SUB * n)
                        dve.wait_ge(y_base, n)
                    nc.vector.scalar_tensor_tensor(x2[:, s, :], wo_banks[s][:, 0:D], tg[:, 0:1], xr[:, s, :],
                                                   ALU.mult, ALU.add).then_inc(x2_set, 1)
                    if s:
                        x2_statistics(s - 1)

                def x2_statistics(s):
                    dve.wait_ge(x2_set, SUB * n + s + 1)
                    subtile_statistics(1, s, x2)
                    if s == SUB - 1:
                        statistics(1, n)

                def outputs_low():
                    for h in range(KT):
                        low_part(oT_lo, oT_hi, turn, n, oT_hi_set, oT_lo_set, h)

                def h_high(f):
                    if f < FT - 1:
                        dve.wait_ge(gelu_done, FT * (n - 1) + f + 1)
                        nc.vector.tensor_copy(h_hi[:, f, :], h_f[:, f, :]).then_inc(h_hi_set, 1)

                def mlp_out(s):
                    dve.wait_ge(f2_done, SUB * (n - 1) + s + 1)
                    dve.wait_ge(y_base, n)
                    yv = y[1 - par][:, s, :]
                    nc.vector.scalar_tensor_tensor(yv, ybank[s % 2][:, 0:D], tg[:, 1:2], yv, ALU.mult, ALU.add
                                                   ).then_inc(y_set, 1)

                def thresholds():
                    dve.wait_ge(wsum_done, 1)
                    nc.vector.tensor_reduce(wsum[:, :], y_ps[:, 0:2 * NW].rearrange("p (w f) -> p w f", w=2),
                                            AX_X, ALU.add).then_inc(thr_step, 1)
                    dve.wait_ge(thr_step, 1)
                    nc.vector.tensor_scalar(wscale[:, :], wsum[:, :], 1.0 / (D * FF), 1e-8, ALU.mult, ALU.max
                                            ).then_inc(thr_step, 1)
                    dve.wait_ge(thr_step, 2)
                    for i, sign in enumerate((0.5, -0.5)):
                        nc.vector.tensor_scalar(thr[:, i, :], wscale[:, :], sign, None, ALU.mult).then_inc(thr_step, 1)
                    dve.wait_ge(thr_step, 4)

                def ternary(w, w_s, i):
                    half = FT * D // 2
                    part = w_s[:, :, :].rearrange("p k n -> p (k n)")[:, i * half:(i + 1) * half]
                    if w or i:
                        dve.wait_ge(tern_set, 2 * w + i)
                    nc.vector.tensor_scalar(tneg, part, thr[:, 1, w:w + 1], None, ALU.is_lt).then_inc(tneg_set, 1)
                    dve.wait_ge(tneg_set, 2 * w + i + 1)
                    nc.vector.scalar_tensor_tensor(part, part, thr[:, 0, w:w + 1], tneg,
                                                   ALU.is_gt, ALU.subtract).then_inc(tern_set, 1)

                def queries_low():
                    hi, lo = first_qT if first else (qT_hi, qT_lo)
                    for h in range(KT):
                        low_part(lo, hi, turn, n + 1, q_hi_set, q_lo_set, h)

                def early_maxima(tile):
                    if second:
                        g0 = sum(EARLY_MAX[t] for t in EARLY_MAX if t < tile)
                        for g in range(g0, g0 + EARLY_MAX[tile]):
                            maxima(g)

                def split(t0, t1):
                    if b and not second:
                        for t in range(t0, t1):
                            p_high(t)

                def statistics_ahead():
                    dve.wait_ge(in_x[par], 16 * (own + 2))
                    for s in range(SUB):
                        subtile_statistics(0, s, xb[par])

                if first:
                    for s in range(SUB):
                        dve.wait_ge(in_first if s < SUB // 2 else in_x[0], 16)
                        subtile_statistics(0, s, xb[0])
                    statistics(0, 0)
                    context_T()
                    dve.wait_ge(shift_set[0], 1)
                    normalize(0, xb[0], 0, SUB)
                split(0, 1)
                if second:
                    ternary(0, W1_s, 1)
                split(1, 2)
                if a:
                    low_part(xT_lo, xT_hi, turn, n + 1, xT_hi_set, xT_lo_set, 0)
                split(2, 3)
                if a:
                    low_part(xT_lo, xT_hi, turn, n + 1, xT_hi_set, xT_lo_set, 1)
                if second:
                    ternary(1, W2_s, 0)
                if first:
                    keys()
                split(3, 5)
                if second:
                    queries_low()
                if prep_v:
                    values()
                early_maxima(5)
                if c and b:
                    low_part(x2T_lo, x2T_hi, mxb, n - 1, x2T_hi_set, x2T_lo_set, 0)
                split(5, 6)
                if c and b:
                    low_part(x2T_lo, x2T_hi, mxb, n - 1, x2T_hi_set, x2T_lo_set, 1)
                if prep_v:
                    value_rows(0, 2)
                early_maxima(6)
                split(6, 7)
                if prep_v:
                    value_rows(2, 3)
                early_maxima(7)
                split(7, 8)
                if b and batch is not None:
                    context_T()
                if b and c and ahead:
                    statistics_ahead()
                split(8, 9)
                if b and c and ahead:
                    statistics(0, n + 2)
                if prep_v:
                    value_rows(3, 4)
                early_maxima(8)
                split(9, NT)
                if b and batch is not None:
                    keys()
                if prep_v:
                    value_rows(4, TH)
                early_maxima(9)
                p_low()
                if not c:
                    statistics_ahead()
                    statistics(0, n + 2)
                if b and batch is not None:
                    keys_high()
                if a and not second:
                    queries_low()
                order = LAST_ORDER if last else ORDER if c else FIRST_ORDER
                for i, kind in enumerate(order):
                    k = order[:i].count(kind)
                    if kind == "M" and a and not (second and k < sum(EARLY_MAX.values())):
                        maxima(k)
                    if kind == "F" and c and not b:
                        h_high(k)
                        if k >= EARLY_AT_END:
                            h_low(k)
                    if kind == "P":
                        if c and not last and k == SUB - 1:
                            for f in range(EARLY if b else FT, FT):
                                h_low(f)
                        if b:
                            head_outputs(k)
                    if kind == "T":
                        for f in range(FT - 1, EARLY_AT_END - 1, -1):
                            h_low(f)
                        outputs_low()
                    if kind == "W":
                        residual(k)
                        if k == SUB - 1:
                            x2_statistics(k)
                    if kind == "Y":
                        if k == SUB - 1:
                            for h in range(KT):
                                low_part(x2T_lo, x2T_hi, mxb, n, x2T_hi_set, x2T_lo_set, h)
                        mlp_out(k)
                        if k == 1:
                            dve.wait_ge(x2T_done, KT * n)
                            dve.wait_ge(shift_set[1], n + 1)
                            normalize(1, x2, SUB // 2, SUB)
                if a:
                    max_parts()
                if c and not last:
                    mlp_out(0)
                if b and a:
                    outputs_low()
                if a:
                    dve.wait_ge(nmT_done, n + 2)
                    nc.vector.tensor_copy(nmT[:, :], mxb[0][0:2 * HEADS, 0:BLK // 2].bitcast(BF16)).then_inc(nmT_set, 1)
                if first:
                    thresholds()
                    ternary(0, W1_s, 0)
                if second:
                    ternary(1, W2_s, 1)
                if c and not last:
                    mlp_out(1)
                if b and a:
                    for s in range(SUB):
                        residual(s)
                    x2_statistics(SUB - 1)
                if c and not last:
                    mlp_out(2)
                    mlp_out(3)
            steps(dve, step)

        @block.tensor
        def _(pe):
            def transposes(src, src_set, bank, blk, done, at_once=False):
                for h in range(KT):
                    for s in range(SUB):
                        if h == 0:
                            pe.wait_ge(src_set, SUB * blk + (SUB if at_once else s + 1))
                        ins = nc.tensor.transpose(bank[h][:, s * P:(s + 1) * P], src[:, s, h * P:(h + 1) * P], ident[:, :])
                    ins.then_inc(done, 1)

            def three(out_, a_hi, a_lo, b_hi, b_lo, first, last):
                nc.tensor.matmul(out_, a_hi, b_hi, start=first, stop=False)
                nc.tensor.matmul(out_, a_lo, b_hi, start=False, stop=False)
                return nc.tensor.matmul(out_, a_hi, b_lo, start=False, stop=last)

            def step(n, par, ahead, a, b, c, own, batch):
                first, second, last = not b and not c, b and not c, b and not a
                prep_v = b and par == 0
                def score_products(t, blk):
                    h, i = divmod(t, TH)
                    if t == 0:
                        if first:
                            pe.wait_ge(b1_set, 1)
                        pe.wait_ge(k_lo_set, (0 if first else own) + 1)
                        pe.wait_ge(q_lo_set, KT * (blk + 1))
                    if t >= 2:
                        pe.wait_ge(exp_done, NT * blk + t - 1)
                    elif c and batch is not None:
                        pe.wait_ge(wt_set, 2 * KT + t + 1)
                    hi, lo = (qT_hi, qT_lo) if c else first_qT
                    cols = slice(i * P, i * P + ROWS[i])
                    o = ring[t % 2][:ROWS[i], :]
                    nc.tensor.matmul(o, K_hi[:, h, cols], hi[:, h, :], start=True, stop=False)
                    nc.tensor.matmul(o, K_hi[:, h, cols], lo[:, h, :], start=False, stop=False)
                    nc.tensor.matmul(o, K_lo[:, h, cols], hi[:, h, :], start=False, stop=False)

                def scores(t0, t1):
                    for t in range(t0, t1):
                        if not second or t >= 2:
                            score_products(t, n)
                        if t == 0:
                            pe.wait_ge(nmT_set, n + 1)
                        h, i = divmod(t, TH)
                        nc.tensor.matmul(ring[t % 2][:ROWS[i], :], headsel[:, h, i * P:i * P + ROWS[i]], nmT[:, :],
                                         start=False, stop=True).then_inc(s_done, 1)

                def query():
                    pe.wait_ge(xT_lo_set, KT * (n + 2))
                    if first:
                        pe.wait_ge(wq_lo_set, 1)
                    for h in range(KT):
                        cols = slice(h * P, (h + 1) * P)
                        for k in range(KT):
                            ins = three(turn[h][:, :], Wq_hi[:, k, cols], Wq_lo[:, k, cols], xT_hi[:, k, :], xT_lo[:, k, :],
                                        k == 0, k == KT - 1)
                        ins.then_inc(q_done, 1)

                def context_T():
                    pe.wait_ge(in_ctx, 16 * (batch + 1))
                    if c:
                        pe.wait_ge(x2T_lo_set, KT * n)
                    for k in range(KT):
                        ins = nc.tensor.transpose(mxb[0][:, k * P:k * P + NK], ctx_s[:, k * P:(k + 1) * P],
                                                  ident[0:NK, 0:NK])
                    ins.then_inc(ctxT_done, 1)

                def keys():
                    pe.wait_ge(ctxT_set, batch + 1)
                    if first:
                        pe.wait_ge(in_wk, 16)
                    for h in range(KT):
                        for k in range(KT):
                            ins = nc.tensor.matmul(mxb[1][:, h * P:h * P + NK], Wk_s[:, k, h * P:(h + 1) * P],
                                                   ctxT[:, k, 0:NK], start=(k == 0), stop=(k == KT - 1))
                    ins.then_inc(kT_done, 1)

                def values():
                    if second:
                        pe.wait_ge(in_wv, 16)
                        pe.wait_ge(thr_step, 1)
                    if c:
                        pe.wait_ge(y_set, SUB * (n - 1))
                    for k in range(KT):
                        ins = nc.tensor.matmul(y_ps[0:NK, 0:D], ctxT[:, k, :], Wv_s[:, k, :],
                                               start=(k == 0), stop=(k == KT - 1))
                    ins.then_inc(vn_done, 1)

                def value_rows(t0, t1):
                    if t0 == 0:
                        pe.wait_ge(vn_set, own + 1)
                        if second:
                            pe.wait_ge(pool_chain, N_CONST)
                    for t in range(t0, t1):
                        if t >= 2:
                            pe.wait_ge(v_set, TH * own + t - 1)
                        h0, h1 = HEADS_OF[t]
                        nc.tensor.matmul(ybank[(t + 1) % 2][:ROWS[t], 0:2 * KT * (h1 - h0) * DH],
                                         keysel[:, t * P:t * P + ROWS[t]],
                                         Vn[:, :, :].rearrange("m w (k h d) -> m (w k) h d", k=KT, h=HH)[:, :, h0:h1, :],
                                         start=True, stop=True).then_inc(v_done, 1)

                def mlp_in(f):
                    if f >= 2:
                        pe.wait_ge(gelu_done, FT * (n - 1) + f - 1)
                    elif b:
                        pe.wait_ge(exp_done, NT * n + NT - 1 + f)
                    cols = slice(f * P, (f + 1) * P)
                    for k in range(KT):
                        if f == 0:
                            pe.wait_ge(x2T_lo_set, KT * (n - 1) + k + 1)
                        for part in (x2T_hi, x2T_lo):
                            ins = nc.tensor.matmul(ring[f % 2][:, :], W1T[:, k, cols], part[:, k, :],
                                                   start=(k == 0 and part is x2T_hi),
                                                   stop=(k == KT - 1 and part is x2T_lo))
                    ins.then_inc(f1_done, 1)

                def attend(s):
                    if s == 0:
                        pe.wait_ge(p_lo_set, NT * (n + 1))
                        if second or last:
                            pe.wait_ge(p_last_lo_set, (NT - P_LAST) * (1 if second else 2))
                        if second:
                            pe.wait_ge(v_ones_set, 2 * TH)
                        pe.wait_ge(v_set, TH * (own + 1))
                    if s >= 2:
                        pe.wait_ge(o_set, SUB * n + s - 1)
                    for h in range(KT):
                        for i in range(TH):
                            r, (h0, h1) = ROWS[i], HEADS_OF[i]
                            for part, w in ((p_hi, 0), (p_lo, 0), (p_hi, 1)):
                                ins = nc.tensor.matmul(
                                    ybank[s % 2][:, (h * HH + h0) * VH:(h * HH + h1) * VH],
                                    part[:r, h * TH + i, s * P:(s + 1) * P],
                                    V_s[:r, i, w, h, h0:h1, :].rearrange("p h c -> p (h c)"),
                                    start=(h == 0 and i == 0 and part is p_hi and w == 0),
                                    stop=(h == KT - 1 and i == TH - 1 and w == 1), skip_group_check=True)
                    ins.then_inc(pv_done, 1)

                def max_scores(g):
                    s, hh = divmod(g, 2 * KT)
                    h, i = divmod(hh, 2)
                    if g == 0:
                        pe.wait_ge(q_hi_set, KT * (n + 2))
                        if batch is not None:
                            pe.wait_ge(k_masked, KT * (batch + 1))
                            pe.wait_ge(k_hi_set, batch + 1)
                    if g == 2:
                        pe.wait_ge(q_lo_set, KT * (n + 2))
                    if g >= 4:
                        pe.wait_ge(mx_red, NMX * (n + 1) + g - 3)
                    hi = first_qT[0] if first else qT_hi
                    nc.tensor.matmul(mx_banks[g % 4][:, 0:HK // 2], hi[:, h, s * P:(s + 1) * P],
                                     K_hi[:, h, i * (HK // 2):(i + 1) * (HK // 2)], start=True, stop=True
                                     ).then_inc(mx_done, 1)

                def project(s):
                    if s == 0:
                        pe.wait_ge(oT_lo_set, KT * (n + 1))
                        if second:
                            pe.wait_ge(wo_lo_set, 1)
                    if s == 3 and a:
                        pe.wait_ge(nmT_set, n + 2)
                    cols = slice(s * P, (s + 1) * P)
                    for k in range(KT):
                        o = wo_banks[s][:, 0:D]
                        nc.tensor.matmul(o, oT_hi[:, k, cols], Wo_hi[:, k, :], start=(k == 0), stop=False)
                        nc.tensor.matmul(o, oT_lo[:, k, cols], Wo_hi[:, k, :], start=False, stop=False)
                        ins = nc.tensor.matmul(o, oT_hi[:, k, cols], Wo_lo[:, k, :], start=False, stop=(k == KT - 1))
                    ins.then_inc(wo_done, 1)

                def mlp_out(s):
                    if s < 2:
                        if b:
                            pe.wait_ge(o_set, SUB * n + s + 3)
                    elif s:
                        pe.wait_ge(y_set, SUB * (n - 1) + s - 1)
                    cols = slice(s * P, (s + 1) * P)
                    early, before, last_before = low_tiles(n, a, b)
                    tiles = [*range(early), *(range(FT - 1, early - 1, -1) if last else range(early, FT))]
                    for i, f in enumerate(tiles):
                        if s == 0 and f < early:
                            pe.wait_ge(h_lo_set, before + f + 1)
                        elif s == 0:
                            pe.wait_ge(h_last_lo_set, last_before + i - early + 1)
                        for part in (h_hi, h_lo):
                            ins = nc.tensor.matmul(ybank[s % 2][:, 0:D], part[:, f, cols], W2T[:, f, :],
                                                   start=(i == 0 and part is h_hi), stop=(i == FT - 1 and part is h_lo))
                    ins.then_inc(f2_done, 1)

                def ternary_T(w):
                    pe.wait_ge(tern_set, 2 * w + 2)
                    if w == 0:
                        pe.wait_ge(exp_done, NT)
                    for g in range(2 * KT * w, 2 * KT * (w + 1)):
                        if g >= 4:
                            pe.wait_ge(wt_set, g - 3)
                        for j in range(4):
                            if g < 2 * KT:
                                src = W1_s[:, g % 2 * 4 + j, g // 2 * P:(g // 2 + 1) * P]
                            else:
                                q = g - 2 * KT
                                ft = q % 2 * 4 + j
                                src = W2_s[:, q // 2, ft * P:(ft + 1) * P]
                            ins = nc.tensor.transpose(wt_banks[g % 4][:, j * P:(j + 1) * P], src, ident[:, :])
                        ins.then_inc(wt_done, 1)

                def max_transposes():
                    pe.wait_ge(nm_set, n + 2)
                    if first:
                        pe.wait_ge(pool_chain, N_CONST)
                    for s in range(SUB):
                        ins = nc.tensor.transpose(mxb[0][0:2 * HEADS, s * P // 2:(s + 1) * P // 2].bitcast(BF16),
                                                  nmb[:, s, :], ident_b[:, :])
                    ins.then_inc(nmT_done, 1)

                def early_maxima(tile):
                    if second:
                        g0 = sum(EARLY_MAX[t] for t in EARLY_MAX if t < tile)
                        for g in range(g0, g0 + EARLY_MAX[tile]):
                            max_scores(g)

                if first:
                    pe.wait_ge(pool_chain, 2)
                    context_T()
                if b:
                    scores(0, 2)
                if a:
                    if c:
                        pe.wait_ge(x2_set, SUB * n)
                    transposes(xn[0], xn_set[0], turn, n + 1, xT_done)
                if first:
                    keys()
                if b:
                    scores(2, 4)
                if c and b:
                    transposes(xn[1], xn_set[1], mxb, n - 1, x2T_done)
                if b:
                    scores(4, 5)
                if second:
                    query()
                if prep_v:
                    values()
                if b:
                    scores(5, 6)
                early_maxima(5)
                if b:
                    scores(6, 7)
                if prep_v:
                    value_rows(0, 2)
                early_maxima(6)
                if b:
                    scores(7, 8)
                if b and batch is not None:
                    context_T()
                if prep_v:
                    value_rows(2, 3)
                early_maxima(7)
                if b:
                    scores(8, 9)
                if prep_v:
                    value_rows(3, 4)
                early_maxima(8)
                if b:
                    scores(9, NT)
                if b and batch is not None:
                    keys()
                if prep_v:
                    value_rows(4, TH)
                early_maxima(9)
                if a and not second:
                    query()
                if first:
                    pe.wait_ge(in_b1, 16)
                    nc.tensor.transpose(ring[0][:, 0:FT], b1_r[:, :], ident[0:FT, 0:FT]).then_inc(b1_done, 1)
                order = LAST_ORDER if last else ORDER if c else FIRST_ORDER
                for i, kind in enumerate(order):
                    k = order[:i].count(kind)
                    if kind == "F" and c:
                        mlp_in(k)
                    if kind == "M" and a and not (second and k < sum(EARLY_MAX.values())):
                        max_scores(k)
                    if kind == "P" and b:
                        attend(k)
                    if kind == "T":
                        transposes(o_s, o_set, turn, n, oT_done)
                    if kind == "W":
                        project(k)
                    if kind == "Y":
                        if k == SUB - 1:
                            transposes(xn[1], xn_set[1], mxb, n, x2T_done, at_once=True)
                        mlp_out(k)
                if c and not last:
                    mlp_out(0)
                if b and a:
                    pe.wait_ge(mx_red, NMX * (n + 2))
                    transposes(o_s, o_set, turn, n, oT_done)
                if first:
                    score_products(0, 0)
                    score_products(1, 0)
                if a:
                    max_transposes()
                if c and not last:
                    mlp_out(1)
                if first:
                    pe.wait_ge(wabs_set, 2 * NW)
                    pe.wait_ge(ones_set, 1)
                    nc.tensor.matmul(y_ps[:, 0:2 * NW], ones[:, :], wabs[:, :, :].rearrange("p w f -> p (w f)"),
                                     start=True, stop=True).then_inc(wsum_done, 1)
                if second:
                    ternary_T(0)
                if b and a:
                    for s in range(SUB):
                        project(s)
                if second:
                    ternary_T(1)
                if c and not last:
                    mlp_out(2)
                    mlp_out(3)
            steps(pe, step)


_INS = ["x", "ctx_1024", "mask_B_ik0", "g_xattn", "g_ffn", "L0_xattn_Wq", "L0_xattn_Wk", "L0_xattn_Wv", "L0_xattn_Wo",
        "L0_ffn_W1", "L0_ffn_b1", "L0_ffn_W2", "L0_ffn_b2"]


def kernel(**inputs):
    import numpy as _np
    import concourse.bacc as _bacc
    from concourse import mybir as _mybir
    from concourse.bass_utils import run_bass_kernel_spmd as _run

    nc = _bacc.Bacc("TRN2", target_bir_lowering=False, num_devices=1)
    arrays, args = {}, []
    for name in _INS:
        if name == "mask_B_ik0":
            continue
        a = _np.ascontiguousarray(inputs[name])
        arrays[f"in_{name}_dram"] = a
        args.append(nc.dram_tensor(f"in_{name}_dram", a.shape, _mybir.dt.from_np(a.dtype), kind="ExternalInput").ap())
    shape = inputs["x"].shape
    args.append(nc.dram_tensor("out_dram", shape, _mybir.dt.float32, kind="ExternalOutput").ap())
    gated_cross_attention_block(nc, *args)
    r = _run(nc, [arrays], core_ids=[0])
    return r.results[0]["out_dram"]
```
